# Optimizing a Trainium2 kernel written in Bass

```python
import numpy as np
import jax
import jax.numpy as jnp

def _softmax(x, axis=-1):
    return jax.nn.softmax(x, axis=axis)

def _gelu(x):
    return jax.nn.gelu(x, approximate=True)

def _silu(x):
    return jax.nn.silu(x)

def _sigmoid(x):
    return jax.nn.sigmoid(x)

def _layernorm(x, axis=-1, eps=1e-05):
    m = jnp.mean(x, axis=axis, keepdims=True)
    v = jnp.var(x, axis=axis, keepdims=True)
    return (x - m) / jnp.sqrt(v + eps)

def _scatter_add(tgt, idx, src, axis=0):
    return tgt.at[idx].add(src)

def _segment_sum(src, seg, n):
    return jax.ops.segment_sum(src, seg, n)
kernel_name = 'mk_macaron_d1_jaxref_r8_f2df39'

def setup_inputs(seed: int=0):
    np.random.seed(seed)
    _w = jnp.asarray

    def _L0_attn_setup():
        import jax, jax.numpy as jnp
        import numpy as np
        D_MODEL, D_STATE, NUM_HEADS = (128, 32, 2)
        D_HEAD = D_STATE // NUM_HEADS
        BATCH, SEQ = (4, 256)
        LN_EPS = 1e-05

        def _ssm(xp, log_neg_lambdas, B_param, C_param):
            b, l, _ = xp.shape
            H, dh = log_neg_lambdas.shape
            xh = xp.reshape(b, l, H, dh)
            lam = jax.nn.sigmoid(log_neg_lambdas)
            u = xh * B_param
            a = jnp.broadcast_to(lam, (b, l, H, dh))

            def comb(e1, e2):
                a1, b1 = e1
                a2, b2 = e2
                return (a1 * a2, a2 * b1 + b2)
            _, h = jax.lax.associative_scan(comb, (a, u), axis=1)
            y = jnp.einsum('blhd,hed->blhe', h, C_param)
            return y.reshape(b, l, H * dh)
        key = jax.random.key(seed)
        ks = jax.random.split(key, 10)
        x = jax.random.normal(ks[0], (BATCH, SEQ, D_MODEL), dtype=jnp.float32)
        log_neg_lambdas = jax.random.normal(ks[1], (NUM_HEADS, D_HEAD), dtype=jnp.float32)
        B_param = jax.random.normal(ks[2], (NUM_HEADS, D_HEAD), dtype=jnp.float32) * 0.1
        C_param = jax.random.normal(ks[3], (NUM_HEADS, D_HEAD, D_HEAD), dtype=jnp.float32) * 0.1
        lim_in = 1.0 / np.sqrt(D_MODEL)
        Wp = jax.random.uniform(ks[4], (D_MODEL, D_STATE), minval=-lim_in, maxval=lim_in, dtype=jnp.float32)
        bp = jax.random.uniform(ks[5], (D_STATE,), minval=-lim_in, maxval=lim_in, dtype=jnp.float32)
        lim_out = 1.0 / np.sqrt(D_STATE)
        Wo = jax.random.uniform(ks[6], (D_STATE, D_MODEL), minval=-lim_out, maxval=lim_out, dtype=jnp.float32)
        bo = jax.random.uniform(ks[7], (D_MODEL,), minval=-lim_out, maxval=lim_out, dtype=jnp.float32)
        ln_gamma = jnp.ones((D_MODEL,), dtype=jnp.float32)
        ln_beta = jnp.zeros((D_MODEL,), dtype=jnp.float32)
        return {'x': x, 'Wp': Wp, 'bp': bp, 'Wo': Wo, 'bo': bo, 'log_neg_lambdas': log_neg_lambdas, 'B_param': B_param, 'C_param': C_param, 'ln_gamma': ln_gamma, 'ln_beta': ln_beta}
    _L0_attn_in = _L0_attn_setup()

    def _L0_ffn_setup():
        import jax, jax.numpy as jnp
        import numpy as np
        D_IN, D_HID = (128, 512)

        def _ternary(key, shape):
            return jax.random.randint(key, shape, -1, 2).astype(jnp.float32)

        def _tlin(x, w, s):
            return jnp.einsum('bsi,oi->bso', x, w) * s
        key = jax.random.key(seed)
        ks = jax.random.split(key, 12)
        inv = lambda fan: 1.0 / np.sqrt(fan).astype(np.float32)
        return {'x': jax.random.normal(ks[0], (4, 256, D_IN), dtype=jnp.float32), 'w1_w': _ternary(ks[1], (D_HID, D_IN)), 'w1_s': jax.random.uniform(ks[2], (D_HID,), dtype=jnp.float32) * inv(D_IN), 'w2_w': _ternary(ks[3], (D_HID, D_IN)), 'w2_s': jax.random.uniform(ks[4], (D_HID,), dtype=jnp.float32) * inv(D_IN), 'h1_w': _ternary(ks[5], (D_HID, D_HID)), 'h1_s': jax.random.uniform(ks[6], (D_HID,), dtype=jnp.float32) * inv(D_HID), 'h2_w': _ternary(ks[7], (D_HID, D_HID)), 'h2_s': jax.random.uniform(ks[8], (D_HID,), dtype=jnp.float32) * inv(D_HID), 'w3_w': _ternary(ks[9], (D_IN, D_HID)), 'w3_s': jax.random.uniform(ks[10], (D_IN,), dtype=jnp.float32) * inv(D_HID)}
    _L0_ffn_in = _L0_ffn_setup()
    _d = {'L0_attn_x': _L0_attn_in['x'], 'L0_attn_Wp': _L0_attn_in['Wp'], 'L0_attn_bp': _L0_attn_in['bp'], 'L0_attn_Wo': _L0_attn_in['Wo'], 'L0_attn_bo': _L0_attn_in['bo'], 'L0_attn_log_neg_lambdas': _L0_attn_in['log_neg_lambdas'], 'L0_attn_B_param': _L0_attn_in['B_param'], 'L0_attn_C_param': _L0_attn_in['C_param'], 'L0_attn_ln_gamma': _L0_attn_in['ln_gamma'], 'L0_attn_ln_beta': _L0_attn_in['ln_beta'], 'L0_ffn_w1_w': _L0_ffn_in['w1_w'], 'L0_ffn_w1_s': _L0_ffn_in['w1_s'], 'L0_ffn_w2_w': _L0_ffn_in['w2_w'], 'L0_ffn_w2_s': _L0_ffn_in['w2_s'], 'L0_ffn_h1_w': _L0_ffn_in['h1_w'], 'L0_ffn_h1_s': _L0_ffn_in['h1_s'], 'L0_ffn_h2_w': _L0_ffn_in['h2_w'], 'L0_ffn_h2_s': _L0_ffn_in['h2_s'], 'L0_ffn_w3_w': _L0_ffn_in['w3_w'], 'L0_ffn_w3_s': _L0_ffn_in['w3_s']}
    _x0 = _d['L0_attn_x']
    _d['L0_attn_x'] = jax.random.normal(jax.random.fold_in(jax.random.key(seed), 1), (16, 256, 128), dtype=_x0.dtype)
    del _x0
    return _d

def reference(L0_attn_x, L0_attn_Wp, L0_attn_bp, L0_attn_Wo, L0_attn_bo, L0_attn_log_neg_lambdas, L0_attn_B_param, L0_attn_C_param, L0_attn_ln_gamma, L0_attn_ln_beta, L0_ffn_w1_w, L0_ffn_w1_s, L0_ffn_w2_w, L0_ffn_w2_s, L0_ffn_h1_w, L0_ffn_h1_s, L0_ffn_h2_w, L0_ffn_h2_s, L0_ffn_w3_w, L0_ffn_w3_s):

    def _L0_attn_ref(x, Wp, bp, Wo, bo, log_neg_lambdas, B_param, C_param, ln_gamma, ln_beta):
        import jax, jax.numpy as jnp
        import numpy as np
        D_MODEL, D_STATE, NUM_HEADS = (128, 32, 2)
        D_HEAD = D_STATE // NUM_HEADS
        BATCH, SEQ = (4, 256)
        LN_EPS = 1e-05

        def _ssm(xp, log_neg_lambdas, B_param, C_param):
            b, l, _ = xp.shape
            H, dh = log_neg_lambdas.shape
            xh = xp.reshape(b, l, H, dh)
            lam = jax.nn.sigmoid(log_neg_lambdas)
            u = xh * B_param
            a = jnp.broadcast_to(lam, (b, l, H, dh))

            def comb(e1, e2):
                a1, b1 = e1
                a2, b2 = e2
                return (a1 * a2, a2 * b1 + b2)
            _, h = jax.lax.associative_scan(comb, (a, u), axis=1)
            y = jnp.einsum('blhd,hed->blhe', h, C_param)
            return y.reshape(b, l, H * dh)
        residual = x
        xp = x @ Wp + bp
        y = _ssm(xp, log_neg_lambdas, B_param, C_param)
        out = y @ Wo + bo
        z = out + residual
        mean = jnp.mean(z, axis=-1, keepdims=True)
        var = jnp.var(z, axis=-1, keepdims=True)
        return (z - mean) / jnp.sqrt(var + LN_EPS) * ln_gamma + ln_beta

    def _L0_ffn_ref(x, w1_w, w1_s, w2_w, w2_s, h1_w, h1_s, h2_w, h2_s, w3_w, w3_s):
        import jax, jax.numpy as jnp
        import numpy as np
        D_IN, D_HID = (128, 512)

        def _ternary(key, shape):
            return jax.random.randint(key, shape, -1, 2).astype(jnp.float32)

        def _tlin(x, w, s):
            return jnp.einsum('bsi,oi->bso', x, w) * s
        h = jax.nn.silu(_tlin(x, w1_w, w1_s)) * _tlin(x, w2_w, w2_s)
        h = jax.nn.gelu(_tlin(h, h1_w, h1_s), approximate=False)
        h = jax.nn.gelu(_tlin(h, h2_w, h2_s), approximate=False)
        return _tlin(h, w3_w, w3_s)
    x = L0_attn_x
    x = x + 0.5 * _L0_ffn_ref(_layernorm(x, axis=-1), L0_ffn_w1_w, L0_ffn_w1_s, L0_ffn_w2_w, L0_ffn_w2_s, L0_ffn_h1_w, L0_ffn_h1_s, L0_ffn_h2_w, L0_ffn_h2_s, L0_ffn_w3_w, L0_ffn_w3_s)
    x = x + _L0_attn_ref(_layernorm(x, axis=-1), L0_attn_Wp, L0_attn_bp, L0_attn_Wo, L0_attn_bo, L0_attn_log_neg_lambdas, L0_attn_B_param, L0_attn_C_param, L0_attn_ln_gamma, L0_attn_ln_beta)
    x = x + 0.5 * _L0_ffn_ref(_layernorm(x, axis=-1), L0_ffn_w1_w, L0_ffn_w1_s, L0_ffn_w2_w, L0_ffn_w2_s, L0_ffn_h1_w, L0_ffn_h1_s, L0_ffn_h2_w, L0_ffn_h2_s, L0_ffn_w3_w, L0_ffn_w3_s)
    return x

_drawn_inputs = setup_inputs


def setup_inputs(seed=0):
    import zlib

    import numpy as np

    out = dict(_drawn_inputs(seed))
    spreads = {'L0_attn_ln_gamma': (1.0, 0.2), 'L0_attn_ln_beta': (0.0, 0.1)}
    factors = {}
    for name, (base, spread) in spreads.items():
        noise = np.random.default_rng([zlib.crc32(name.encode()), seed]).standard_normal(out[name].shape)
        drawn = base * np.exp(spread * noise) if base else spread * noise
        out[name] = jnp.asarray(drawn.astype(out[name].dtype))
    for name, factor in factors.items():
        out[name] = (out[name] * factor).astype(out[name].dtype)
    return out
```

```python
import concourse.bass as bass
from concourse import mybir
from contextlib import ExitStack

f32 = mybir.dt.float32
f32r = mybir.dt.float32r
i32 = mybir.dt.int32
ALU = mybir.AluOpType
ACT = mybir.ActivationFunctionType
AX = mybir.AxisListType

P = 128
BATCH, SEQ = 16, 256
TOK = 512
NT = BATCH * SEQ // TOK
SUB = TOK // P
SB = TOK // SEQ
HID = 512
KB = HID // P
CH = 32
HEADS, DH = 2, 16
EPS = 1e-5
UNITS = 2 * NT

W1, W2 = 0, HID
H1, H2 = 2 * HID, 2 * HID + KB * HID
W3 = 2 * HID + 2 * KB * HID
WCOLS = W3 + KB * P
SECTIONS = [(W1, W2), (W2, H1), (H1, H2), (H2, W3), (W3, WCOLS)]


def b_unit(t):
    if isinstance(t, int) and t >= NT - 2:
        return UNITS - NT + t
    return t * 2 + 3


IDLE = 6
POOL_STEPS, DVE_STEPS = 14, 48


class Steps:

    def __init__(self, eng, sem):
        self.eng, self.sem, self.base, self.n = eng, sem, 0, 0

    def add(self, ins):
        self.n += 1
        ins.then_inc(self.sem, 1)
        return self.base + self.n

    def wait(self, value):
        self.eng.wait_ge(self.sem, value)

    def enter(self, i, first, per_turn):
        self.start, self.first, self.per_turn = self.base + self.n, first, per_turn
        self.base, self.n = (i - first) * per_turn + self.start, 0

    def leave(self, turns):
        assert self.n == self.per_turn, (self.n, self.per_turn)
        self.base, self.n = self.start + turns * self.per_turn, 0


class Phase:

    def __init__(self, n, start=True, finish=None, mix=None, prepare=None, late=False):
        self.n, self.start, self.finish, self.mix, self.prepare, self.late = n, start, finish, mix, prepare, late


HEAD = [
    Phase(0, prepare=("A", 1)),
    Phase(1, finish=("A", 0), prepare=("A", 2)),
    Phase(2, finish=("A", 1), mix=0, prepare=("B", 0), late=True),
    Phase(3, finish=("A", 2), mix=1, prepare=("A", 3)),
]
LOOP_FIRST, LOOP_END = 2, NT - 2


def loop_phases(i):
    return [
        Phase(i * 2, finish=("B", i - 2), mix=i, prepare=("B", i - 1)),
        Phase(i * 2 + 1, finish=("A", i + 1), prepare=("A", i + 2)),
    ]


TAIL = [
    Phase(2 * NT - 4, finish=("B", NT - 4), mix=NT - 2, prepare=("B", NT - 3)),
    Phase(2 * NT - 3, finish=("A", NT - 1), prepare=("B", NT - 2)),
    Phase(2 * NT - 2, finish=("B", NT - 3), mix=NT - 1, prepare=("B", NT - 1), late=True),
    Phase(2 * NT - 1, finish=("B", NT - 2)),
    Phase(2 * NT, start=False, finish=("B", NT - 1)),
]


def tile_of(a, t):
    return a[:, t] if isinstance(t, int) else a[:, bass.ds(t, 1)].rearrange("p o s f -> p (o s) f")


def above(value, least):
    return not isinstance(value, int) or value >= least


def macaron_kernel(nc, x, weights, scales, rows, wp, cmat, wo, chan, out):
    ctx = ExitStack()
    with ctx:
        def sb(name, shape, dt=f32):
            return ctx.enter_context(nc.sbuf_tensor(name, shape, dt))

        def pb(name):
            return ctx.enter_context(nc.psum_tensor(name, [P, TOK], f32))

        def sem(name):
            return ctx.enter_context(nc.semaphore(name))

        w_raw = sb("w_raw", [P, WCOLS])
        w_hi = sb("w_hi", [P, WCOLS], f32r)
        w_lo = sb("w_lo", [P, WCOLS], f32r)
        w_odd = sb("w_odd", [P, 2, HID])
        odd_cols = sb("odd_cols", [P, WCOLS // HID])
        odd_col = sb("odd_col", [P, 1])
        odd_flag = sb("odd_flag", [1, 1], i32)
        ones_col = sb("ones_col", [P, 1])
        scale_in = sb("scale_in", [P, 5, KB])
        half_s1 = sb("half_s1", [P, KB])
        gate_s = sb("gate_s", [P, KB])
        half_s3 = sb("half_s3", [P, 1])
        row_in = sb("row_in", [P, 3, P])
        bo_bc, gamma_bc, beta_bc = (row_in[:, r, :] for r in range(3))
        bo4 = sb("bo4", [P, SUB, P])
        beta4 = sb("beta4", [P, SUB, P])
        ident = sb("ident", [P, P])
        wp_pad = sb("wp_pad", [P, SB, P])
        c_diag = sb("c_diag", [CH, SB, CH])
        wo_in = sb("wo_in", [CH, P])
        cwo = sb("cwo", [P, SB, P])
        chan_in = sb("chan_in", [SB * CH, 3])
        lam_t = sb("lam_t", [SB * CH, 1])
        lam = sb("lam", [SB * CH, SEQ])
        pool_idle, dve_idle = sb("pool_idle", [P, IDLE]), sb("dve_idle", [P, IDLE])
        minus_half = sb("minus_half", [P, SUB])

        x_all = sb("x_all", [P, NT, SUB, P])
        x2_all = sb("x2_all", [P, NT, SUB, P])
        x1 = sb("x1", [P, SUB, P])
        x2 = sb("x2", [P, SUB, P])
        xn_a = sb("xn_a", [P, SUB, P])
        xn_b = sb("xn_b", [P, SUB, P])
        z = sb("z", [P, SUB, P])
        z_bo = sb("z_bo", [P, SUB, P])
        x1_beta = sb("x1_beta", [P, SUB, P])
        mixed = sb("mixed", [P, SUB, P])
        centred = sb("centred", [P, SUB, P])
        out_sb = sb("out_sb", [P, SUB, P])
        stats = sb("stats", [P, SUB, 6])
        ln = {k: dict(mv=sb(f"mv_{k}", [P, SUB, 2]), var=sb(f"var_{k}", [P, SUB]), neg=sb(f"neg_{k}", [P, SUB]),
                      rstd=sb(f"rstd_{k}", [P, SUB])) for k in ("a", "z", "mix", "b")}
        xt_hi = sb("xt_hi", [P, TOK], f32r)
        xt_lo = sb("xt_lo", [P, TOK], f32r)
        z_t = sb("z_t", [P, TOK])
        tanh_g = sb("tanh_g", [P, 2, TOK])
        gate = sb("gate", [P, 2, TOK])
        h1f = sb("h1f", [P, 2, TOK])
        h1_hi = sb("h1_hi", [P, KB, TOK], f32r)
        h1_lo = sb("h1_lo", [P, KB, TOK], f32r)
        hf = sb("hf", [P, 2, TOK])
        h2_hi = sb("h2_hi", [P, KB, TOK], f32r)
        h2_lo = sb("h2_lo", [P, KB, TOK], f32r)
        h3_hi = sb("h3_hi", [P, KB, TOK], f32r)
        h3_lo = sb("h3_lo", [P, KB, TOK], f32r)
        y_t = sb("y_t", [P, TOK])
        u_in = sb("u_in", [SB * CH, SEQ])
        state = sb("state", [P, SEQ])

        ps_g = [pb(f"ps_g{j}") for j in range(2)]
        ps_u = [pb(f"ps_u{j}") for j in range(2)]
        ps_h = [pb(f"ps_h{j}") for j in range(2)]
        ps_y = pb("ps_y")
        ps_m = pb("ps_m")

        s_x = [sem(f"x_loaded{t}") for t in range(2)]
        s_xrest = sem("x_rest_loaded")
        s_w = [sem(f"weights_loaded{j}") for j in range(len(SECTIONS))]
        s_par = sem("params_loaded")
        s_zero = sem("zeros_written")
        s_pad = sem("padded_loaded")
        s_ident = sem("ident_ready")
        s_const = sem("dve_consts_ready")
        s_whi_v = sem("w_hi_by_dve")
        s_whi_a = sem("w_hi_by_act")
        s_wlo = sem("w_lo_ready")
        s_odd = sem("odd_ready")
        s_oddsum = sem("odd_sum_ready")
        s_flag = sem("flag_ready")
        s_half = sem("half_scales_ready")
        s_cwo_sb = sem("cwo_ready")
        s_cwo = sem("cwo_product_ready")
        s_lam = sem("lam_tanh_ready")
        s_xn_a = sem("xn_a_ready")
        s_xn_b = sem("xn_b_ready")
        s_xt = sem("xt_transposed")
        s_xt_hi = sem("xt_hi_ready")
        s_xt_lo = sem("xt_lo_ready")
        s_l1 = sem("l1_done")
        s_tanh = sem("tanh_ready")
        s_h1f = sem("h1f_ready")
        s_h1_hi = sem("h1_hi_ready")
        s_h1_lo = sem("h1_lo_ready")
        s_hid = sem("hidden_done")
        s_hid_hi = sem("hidden_hi_ready")
        s_hid_f = sem("hidden_full_ready")
        s_hid_lo = sem("hidden_lo_ready")
        s_y = sem("y_done")
        s_y_t = sem("y_scaled")
        s_yb = sem("y_transposed")
        s_fin = sem("y_added")
        s_z_st = sem("z_stats_ready")
        s_z = sem("z_ready")
        s_zbo = sem("z_bo_ready")
        s_x1b = sem("x1_beta_ready")
        s_zt = sem("z_transposed")
        s_zt_sb = sem("z_t_ready")
        s_xp = sem("xp_done")
        s_state = sem("state_ready")
        s_mix = sem("mix_product_done")
        s_mixed = sem("mixed_ready")
        s_mix_st = sem("mix_stats_ready")
        s_mix_r = sem("mix_rstd_ready")
        s_x2 = sem("x2_ready")
        s_b_st = sem("b_stats_ready")
        s_a_st = sem("a_stats_ready")
        s_a_r = sem("a_rstd_ready")
        s_stored = sem("out_stored")
        s_dve = sem("dve_steps")
        s_pool = sem("pool_steps")

        block = ctx.enter_context(nc.Block())

        @block.sync
        def _(sp):
            sp.dma_start(x_all[:, 0], x[:, 0]).then_inc(s_x[0], 16)
            sp.dma_start(w_raw[:, W1:W2], weights[:, W1:W2]).then_inc(s_w[0], 16)
            sp.dma_start(w_raw[:, W2:H1], weights[:, W2:H1]).then_inc(s_w[1], 16)
            sp.dma_start(scale_in[:], scales).then_inc(s_par, 16)
            sp.dma_start(w_raw[:, H1:H2], weights[:, H1:H2]).then_inc(s_w[2], 16)
            sp.dma_start(x_all[:, 1], x[:, 1]).then_inc(s_x[1], 16)
            sp.dma_start(w_raw[:, H2:W3], weights[:, H2:W3]).then_inc(s_w[3], 16)
            sp.dma_start(w_raw[:, W3:WCOLS], weights[:, W3:WCOLS]).then_inc(s_w[4], 16)
            for r in range(3):
                sp.dma_start(row_in[:, r, :], rows[r:r + 1, :].to_broadcast([P, P])).then_inc(s_par, 16)
            for b in range(SB):
                sp.dma_start(chan_in[CH * b:CH * b + CH, :], chan).then_inc(s_par, 16)
            sp.dma_start(wo_in[:], wo).then_inc(s_par, 16)
            sp.wait_ge(s_zero, 2)
            for b in range(SB):
                sp.dma_start(wp_pad[:, b, CH * b:CH * b + CH], wp).then_inc(s_pad, 16)
                for h in range(HEADS):
                    sp.dma_start(c_diag[DH * h:DH * h + DH, b, DH * h:DH * h + DH], cmat[h]).then_inc(s_pad, 16)
            sp.dma_start(x_all[:, 2:NT], x[:, 2:NT]).then_inc(s_xrest, 16)

            def store(t):
                sp.wait_ge(s_fin, b_unit(t) + 1)
                sp.dma_start(tile_of(out, t), out_sb[:]).then_inc(s_stored, 16)

            with sp.Fori(0, NT - 2) as t:
                store(t)
            store(NT - 2)
            store(NT - 1)
            sp.wait_ge(s_stored, 16 * NT)

        N_PAR = 16 * (1 + 3 + SB + 1)
        N_PAD = 16 * SB * (1 + HEADS)

        @block.gpsimd
        def _(pool):
            st = Steps(pool, s_pool)
            nc.gpsimd.memset(wp_pad[:], 0.0).then_inc(s_zero, 1)
            nc.gpsimd.memset(c_diag[:], 0.0).then_inc(s_zero, 1)
            v = st.add(nc.gpsimd.memset(ident[:], 0.0))
            m = st.add(nc.gpsimd.memset(minus_half[:], -0.5))
            st.wait(v)
            nc.gpsimd.affine_select(out=ident[:], in_=ident[:], compare_op=ALU.not_equal, fill=1.0, base=0,
                                    pattern=[[-1, P]], channel_multiplier=1).then_inc(s_ident, 1)
            st.wait(m)


            idle = [0]

            def wait_alone(semaphore, value):
                pool.wait_ge(semaphore, value)
                if not isinstance(value, int):
                    idle[0] = (idle[0] + 1) % IDLE
                    nc.gpsimd.tensor_tensor(pool_idle[:, idle[0]:idle[0] + 1], minus_half[:, 0:1],
                                            minus_half[:, 1:2], ALU.add)


            def rstd(kind):
                c = ln[kind]
                v = st.add(nc.gpsimd.tensor_scalar(c["var"][:], c["mv"][:, :, 1], EPS, None, ALU.add))
                st.wait(v)
                return nc.gpsimd.tensor_tensor(c["rstd"][:], c["var"][:], minus_half[:], ALU.pow)

            def negate_mean(kind):
                c = ln[kind]
                return nc.gpsimd.tensor_scalar(c["neg"][:], c["mv"][:, :, 0], -1.0, None, ALU.mult)

            def normalise(kind, dst, src):
                c = ln[kind]
                for s in range(SUB):
                    last = nc.gpsimd.tensor_scalar(dst[:, s, :], src[:, s, :], c["neg"][:, s:s + 1],
                                                   c["rstd"][:, s:s + 1], ALU.add, ALU.mult)
                    if s < SUB - 1:
                        st.add(last)
                return last

            def rstd_a(count):
                wait_alone(s_a_st, count)
                rstd("a").then_inc(s_a_r, 1)

            def phase(ph):
                n = ph.n
                for k in range(KB):
                    if ph.start:
                        pool.wait_ge(s_h1_hi, n * KB + k + 1)
                        if k == 0 and above(n, 1):
                            pool.wait_ge(s_hid, n * 8 - 4)
                        nc.gpsimd.tensor_tensor(h1_lo[:, k, :], h1f[:, k % 2, :], h1_hi[:, k, :].bitcast(f32),
                                                ALU.subtract).then_inc(s_h1_lo, 1)
                    if k == 0 and ph.prepare and ph.prepare[0] == "A":
                        rstd_a(ph.prepare[1] + 1)
                if ph.mix is not None:
                    t = ph.mix
                    wait_alone(s_mix_st, t + 1)
                    rstd("mix").then_inc(s_mix_r, 1)
                    if above(t, 1):
                        pool.wait_ge(s_xt, b_unit(t - 1) + 1)
                    wait_alone(s_b_st, t + 1)
                    st.add(negate_mean("b"))
                    v = st.add(rstd("b"))
                    wait_alone(st.sem, v)
                    normalise("b", xn_b, x2).then_inc(s_xn_b, 1)
                if ph.finish and ph.finish[0] == "A":
                    t = ph.finish[1]
                    if above(t, 1):
                        pool.wait_ge(s_zt, t)
                    wait_alone(s_z_st, t + 1)
                    st.add(negate_mean("z"))
                    v = st.add(rstd("z"))
                    wait_alone(st.sem, v)
                    normalise("z", z, x1[:]).then_inc(s_z, 1)
                    if above(t, 1):
                        pool.wait_ge(s_x2, t)
                    nc.gpsimd.tensor_tensor(x1_beta[:], x1[:], beta4[:], ALU.add).then_inc(s_x1b, 1)
                    pool.wait_ge(s_z, t + 1)
                    nc.gpsimd.tensor_tensor(z_bo[:], z[:], bo4[:], ALU.add).then_inc(s_zbo, 1)

            rstd_a(1)
            pool.wait_ge(s_flag, 1)
            odd = pool.value_load(odd_flag[0:1, 0:1])
            with pool.If(odd != 0):
                for c in range(0, WCOLS, HID):
                    part = slice(c, c + HID)
                    nc.gpsimd.tensor_tensor(w_lo[:, part], w_raw[:, part], w_hi[:, part].bitcast(f32),
                                            ALU.subtract).then_inc(s_wlo, 1)
            pool.wait_ge(s_const, 1)
            for ph in HEAD:
                phase(ph)
            with pool.Fori(LOOP_FIRST, LOOP_END) as i:
                st.enter(i, LOOP_FIRST, POOL_STEPS)
                for ph in loop_phases(i):
                    phase(ph)
                st.leave(LOOP_END - LOOP_FIRST)
            for ph in TAIL:
                phase(ph)

        @block.scalar
        def _(act):
            act.wait_ge(s_par, N_PAR)
            nc.scalar.activation(lam_t[:], chan_in[:, 0:1], ACT.Gelu).then_inc(s_lam, 1)
            act.wait_ge(s_lam, 1)
            nc.scalar.activation(lam_t[:], chan_in[:, 0:1], ACT.Tanh, scale=0.5).then_inc(s_lam, 1)

            def xt_to_hi(n):
                act.wait_ge(s_xt, n + 1)
                nc.scalar.activation(xt_hi[:], ps_m[:], ACT.Copy).then_inc(s_xt_hi, 1)

            def gelu(q, k, scale, dst_hi):
                act.wait_ge(s_hid, q + 1)
                nc.scalar.activation(dst_hi, ps_h[k % 2][:], ACT.Gelu, scale=scale).then_inc(s_hid_hi, 1)
                if above(q, 2):
                    act.wait_ge(s_hid_lo, q - 1)
                nc.scalar.activation(hf[:, k % 2, :], ps_h[k % 2][:], ACT.Gelu, scale=scale).then_inc(s_hid_f, 1)

            def phase(ph):
                n = ph.n
                for k in range(KB):
                    if ph.start:
                        q = n * KB + k
                        act.wait_ge(s_l1, q + 1)
                        if above(q, 2):
                            act.wait_ge(s_h1f, q - 1)
                        nc.scalar.activation(tanh_g[:, k % 2, :], ps_g[k % 2][:], ACT.Tanh,
                                             scale=half_s1[:, k:k + 1]).then_inc(s_tanh, 1)
                    if ph.finish:
                        gelu(n * 8 - 4 + k, k, scale_in[:, 3, k:k + 1], h3_hi[:, k, :])
                    if k == 0 and ph.mix is not None:
                        act.wait_ge(s_zt, ph.mix + 1)
                        nc.scalar.activation(z_t[:], ps_m[:], ACT.Copy).then_inc(s_zt_sb, 1)
                    if ph.start:
                        act.wait_ge(s_h1f, q + 1)
                        nc.scalar.activation(h1_hi[:, k, :], h1f[:, k % 2, :], ACT.Copy).then_inc(s_h1_hi, 1)
                if ph.start:
                    for k in range(KB):
                        gelu(n * 8 + k, k, scale_in[:, 2, k:k + 1], h2_hi[:, k, :])
                        if k == 1 and ph.finish:
                            scale_y(n)
                        if k == (KB - 1 if ph.late else KB - 2) and ph.prepare:
                            xt_to_hi(n + 1)
                else:
                    scale_y(n)

            def scale_y(n):
                act.wait_ge(s_y, n)
                nc.scalar.activation(y_t[:], ps_y[:], ACT.Copy, scale=half_s3[:]).then_inc(s_y_t, 1)

            for j in range(2, len(SECTIONS)):
                a, b = SECTIONS[j]
                act.wait_ge(s_w[j], 16)
                nc.scalar.activation(w_hi[:, a:b], w_raw[:, a:b], ACT.Copy).then_inc(s_whi_a, 1)
            act.wait_ge(s_half, 1)
            xt_to_hi(0)
            for ph in HEAD:
                phase(ph)
            with act.Fori(LOOP_FIRST, LOOP_END) as i:
                for ph in loop_phases(i):
                    phase(ph)
            for ph in TAIL:
                phase(ph)

        @block.vector
        def _(dve):
            st = Steps(dve, s_dve)

            idle = [0]

            def wait_alone(semaphore, value):
                dve.wait_ge(semaphore, value)
                if not isinstance(value, int):
                    idle[0] = (idle[0] + 1) % IDLE
                    nc.vector.memset(dve_idle[:, idle[0]:idle[0] + 1], 0.0)


            def layer_stats(kind, src, first_wait=None):
                for s in range(SUB):
                    v = st.add(nc.vector.bn_stats(stats[:, s, :], src(s)))
                wait_alone(st.sem, v)
                for s in range(SUB):
                    last = nc.vector.bn_aggr(ln[kind]["mv"][:, s, :], stats[:, s, :])
                    if s < SUB - 1:
                        st.add(last)
                return last

            def stats_a(t):
                src = tile_of(x_all, t)
                layer_stats("a", lambda s: src[:, s, :]).then_inc(s_a_st, 1)

            def normalise_a(t):
                dve.wait_ge(s_a_r, t + 1)
                dve.wait_ge(s_a_st, t + 1)
                src = tile_of(x_all, t)
                for s in range(SUB):
                    last = nc.vector.tensor_scalar(xn_a[:, s, :], src[:, s, :], ln["a"]["mv"][:, s, 0:1],
                                                   ln["a"]["rstd"][:, s:s + 1], ALU.subtract, ALU.mult)
                    if s < SUB - 1:
                        st.add(last)
                last.then_inc(s_xn_a, 1)

            def xt_to_lo(n):
                dve.wait_ge(s_xt_hi, n + 1)
                nc.vector.tensor_tensor(xt_lo[:], ps_m[:], xt_hi[:].bitcast(f32), ALU.subtract).then_inc(s_xt_lo, 1)

            def hidden_lo(q, k, hi, lo):
                dve.wait_ge(s_hid_f, q + 1)
                nc.vector.tensor_tensor(lo, hf[:, k % 2, :], hi.bitcast(f32), ALU.subtract).then_inc(s_hid_lo, 1)

            def recur(t):
                dve.wait_ge(s_xp, t + 1)
                v = st.add(nc.vector.tensor_scalar(u_in[:], ps_m[0:SB * CH, 0:SEQ], chan_in[:, 2:3], chan_in[:, 1:2],
                                                   ALU.add, ALU.mult))
                st.wait(v)
                nc.vector.tensor_tensor_scan(state[0:SB * CH, :], lam[:], u_in[:], 0.0, ALU.mult,
                                             ALU.add).then_inc(s_state, 1)

            def mixer_sum(t):
                dve.wait_ge(s_mix, t + 1)
                dve.wait_ge(s_zbo, t + 1)
                nc.vector.tensor_tensor(mixed[:], ps_m[:].rearrange("p (s f) -> p s f", s=SUB), z_bo[:],
                                        ALU.add).then_inc(s_mixed, 1)
                dve.wait_ge(s_mixed, t + 1)
                layer_stats("mix", lambda s: mixed[:, s, :]).then_inc(s_mix_st, 1)

            def mixer_norm(t):
                dve.wait_ge(s_mix_r, t + 1)
                dve.wait_ge(s_mix_st, t + 1)
                for s in range(SUB):
                    v = st.add(nc.vector.scalar_tensor_tensor(
                        out=centred[:, s, :], in0=mixed[:, s, :], scalar=ln["mix"]["mv"][:, s, 0:1], in1=gamma_bc,
                        op0=ALU.subtract, op1=ALU.mult))
                dve.wait_ge(s_x1b, t + 1)
                st.wait(v)
                if above(t, 1):
                    dve.wait_ge(s_xn_b, t)
                for s in range(SUB):
                    last = nc.vector.scalar_tensor_tensor(
                        out=x2[:, s, :], in0=centred[:, s, :], scalar=ln["mix"]["rstd"][:, s:s + 1],
                        in1=x1_beta[:, s, :], op0=ALU.mult, op1=ALU.add)
                    if s < SUB - 1:
                        st.add(last)
                last.then_inc(s_x2, 1)
                dve.wait_ge(s_x2, t + 1)
                layer_stats("b", lambda s: x2[:, s, :]).then_inc(s_b_st, 1)
                st.add(nc.vector.tensor_copy(tile_of(x2_all, t), x2[:]))

            def finish(kind, t, n):
                dve.wait_ge(s_yb, n)
                y = ps_y[:].rearrange("p (s f) -> p s f", s=SUB)
                if kind == "A":
                    if above(t, 1):
                        dve.wait_ge(s_x1b, t)
                    nc.vector.tensor_tensor(x1[:], y, tile_of(x_all, t), ALU.add).then_inc(s_fin, 1)
                else:
                    if above(t, 1):
                        dve.wait_ge(s_stored, t * 16)
                    nc.vector.tensor_tensor(out_sb[:], y, tile_of(x2_all, t), ALU.add).then_inc(s_fin, 1)

            def finish_stats(n):
                dve.wait_ge(s_fin, n)
                layer_stats("z", lambda s: x1[:, s, :]).then_inc(s_z_st, 1)

            def phase(ph):
                n = ph.n
                for k in range(KB):
                    if ph.start:
                        q = n * KB + k
                        dve.wait_ge(s_tanh, q + 1)
                        v = st.add(nc.vector.scalar_tensor_tensor(
                            out=gate[:, k % 2, :], in0=tanh_g[:, k % 2, :], scalar=1.0, in1=ps_g[k % 2][:],
                            op0=ALU.add, op1=ALU.mult))
                    if ph.finish and k:
                        hidden_lo(n * 8 - 5 + k, k - 1, h3_hi[:, k - 1, :], h3_lo[:, k - 1, :])
                    if ph.start:
                        st.wait(v)
                        if above(q, 2):
                            dve.wait_ge(s_h1_hi, q - 1)
                            dve.wait_ge(s_h1_lo, q - 1)
                        nc.vector.scalar_tensor_tensor(
                            out=h1f[:, k % 2, :], in0=ps_u[k % 2][:], scalar=gate_s[:, k:k + 1], in1=gate[:, k % 2, :],
                            op0=ALU.mult, op1=ALU.mult).then_inc(s_h1f, 1)
                    if k == 0 and ph.prepare and ph.prepare[0] == "A":
                        ta = ph.prepare[1]
                        if not isinstance(ta, int) or ta >= 2:
                            dve.wait_ge(s_xrest, 16)
                        else:
                            dve.wait_ge(s_x[ta], 16)
                        stats_a(ta)
                    if k == 2 and ph.mix is not None:
                        recur(ph.mix)
                    if k == 2 and ph.prepare and ph.prepare[0] == "A":
                        normalise_a(ph.prepare[1])
                if ph.finish:
                    hidden_lo(n * 8 - 1, KB - 1, h3_hi[:, KB - 1, :], h3_lo[:, KB - 1, :])
                if ph.start:
                    for k in range(KB):
                        if k == KB - 1:
                            if ph.prepare and not ph.late:
                                xt_to_lo(n + 1)
                            if ph.finish:
                                finish(*ph.finish, n)
                        hidden_lo(n * 8 + k, k, h2_hi[:, k, :], h2_lo[:, k, :])
                        if k == 0 and ph.mix is not None:
                            mixer_sum(ph.mix)
                        if k == 1 and ph.mix is not None:
                            mixer_norm(ph.mix)
                    if ph.finish and ph.finish[0] == "A":
                        finish_stats(n)
                    if ph.prepare and ph.late:
                        xt_to_lo(n + 1)
                else:
                    finish(*ph.finish, n)

            st_ones = st.add(nc.vector.memset(ones_col[:], 1.0))
            st.add(nc.vector.memset(state[:], 0.0))
            st_zero = st.add(nc.vector.memset(cwo[:], 0.0))
            st_lam = st.add(nc.vector.memset(lam[:], 1.0))
            dve.wait_ge(s_x[0], 16)
            stats_a(0)
            odd_at = []

            def check_section(j):
                a, b = SECTIONS[j]
                for c in range(a, b, HID):
                    if len(odd_at) > 1:
                        st.wait(odd_at[-2])
                    odd_at.append(st.add(nc.vector.scalar_tensor_tensor(
                        out=w_odd[:, c // HID % 2, :], in0=w_raw[:, c:c + HID], scalar=1.0, in1=w_hi[:, c:c + HID].bitcast(f32),
                        op0=ALU.mult, op1=ALU.not_equal, accum_out=odd_cols[:, c // HID:c // HID + 1])))

            for j in range(2):
                a, b = SECTIONS[j]
                dve.wait_ge(s_w[j], 16)
                nc.vector.tensor_copy(w_hi[:, a:b], w_raw[:, a:b]).then_inc(s_whi_v, 1)
            normalise_a(0)
            dve.wait_ge(s_whi_v, 2)
            check_section(0)
            check_section(1)
            dve.wait_ge(s_par, N_PAR)
            v = st.add(nc.vector.tensor_scalar(half_s1[:], scale_in[:, 0, :], 0.5, None, ALU.mult))
            nc.vector.tensor_scalar(half_s3[:], scale_in[:, 4, 0:1], 0.5, None, ALU.mult).then_inc(s_half, 1)
            st.wait(v)
            st.add(nc.vector.tensor_tensor(gate_s[:], half_s1[:], scale_in[:, 1, :], ALU.mult))
            st.add(nc.vector.tensor_copy(bo4[:], bo_bc.unsqueeze(1).broadcast_to([P, SUB, P])))
            nc.vector.tensor_copy(beta4[:], beta_bc.unsqueeze(1).broadcast_to([P, SUB, P])).then_inc(s_const, 1)
            dve.wait_ge(s_lam, 2)
            v = st.add(nc.vector.tensor_scalar(lam_t[:], lam_t[:], 0.5, 0.5, ALU.mult, ALU.add))
            st.wait(v)
            st.add(nc.vector.tensor_scalar(lam[:], lam[:], lam_t[:], None, ALU.mult))
            xt_to_lo(0)
            dve.wait_ge(s_cwo, 1)
            for b in range(SB):
                rows_b = slice(CH * b, CH * b + CH)
                last = nc.vector.tensor_copy(cwo[rows_b, b, :], ps_y[rows_b, 0:P])
                if b < SB - 1:
                    st.add(last)
            last.then_inc(s_cwo_sb, 1)
            for j in range(2, len(SECTIONS)):
                dve.wait_ge(s_whi_a, j - 1)
                check_section(j)
            st.wait(st.base + st.n)
            nc.vector.reduce_sum(odd_col[:], odd_cols[:], AX.X).then_inc(s_odd, 1)
            dve.wait_ge(s_oddsum, 1)
            nc.vector.tensor_copy(odd_flag[:], ps_y[0:1, 0:1]).then_inc(s_flag, 1)

            for ph in HEAD:
                phase(ph)
            with dve.Fori(LOOP_FIRST, LOOP_END) as i:
                st.enter(i, LOOP_FIRST, DVE_STEPS)
                for ph in loop_phases(i):
                    phase(ph)
                st.leave(LOOP_END - LOOP_FIRST)
            for ph in TAIL:
                phase(ph)

        @block.tensor
        def _(pe):
            def transpose4(dst, src):
                for s in range(SUB):
                    last = nc.tensor.transpose(dst[:, s * P:(s + 1) * P], src(s), ident[:])
                return last

            def product(dst, wcol, hi, lo, first, final, exact, lo_wait=None):
                w = w_hi[:, wcol:wcol + P]
                nc.tensor.matmul(dst, w, hi, start=first, stop=False)
                if not exact:
                    nc.tensor.matmul(dst, w_lo[:, wcol:wcol + P], hi, start=False, stop=False)
                if lo_wait:
                    pe.wait_ge(*lo_wait)
                last = nc.tensor.matmul(dst, w, lo, start=False, stop=final and exact)
                if not exact:
                    last = nc.tensor.matmul(dst, w_lo[:, wcol:wcol + P], lo, start=False, stop=final)
                return last

            def transpose_input(n, src, ready, count):
                pe.wait_ge(ready, count)
                transpose4(ps_m, lambda s: src[:, s, :]).then_inc(s_xt, 1)

            def layer1(n, k, exact):
                q = n * KB + k
                if k == 0:
                    pe.wait_ge(s_xt_hi, n + 1)
                if above(q, 2):
                    pe.wait_ge(s_h1f, q - 1)
                product(ps_g[k % 2][:], W1 + k * P, xt_hi[:], xt_lo[:], True, True, exact,
                        (s_xt_lo, n + 1) if k == 0 else None)
                product(ps_u[k % 2][:], W2 + k * P, xt_hi[:], xt_lo[:], True, True, exact).then_inc(s_l1, 1)

            def hidden(q, k, w0, hi, lo, hi_at, lo_at, exact):
                if above(q, 2):
                    pe.wait_ge(s_hid_f, q - 1)
                for j in range(KB):
                    if k == 0:
                        pe.wait_ge(hi_at[0], hi_at[1] + j + 1)
                    last = product(ps_h[k % 2][:], w0 + j * HID + k * P, hi[:, j, :], lo[:, j, :],
                                   j == 0, j == KB - 1, exact,
                                   (lo_at[0], lo_at[1] + j + 1) if k == 0 else None)
                last.then_inc(s_hid, 1)

            def last_layer(n, exact):
                if above(n, 2):
                    pe.wait_ge(s_fin, n - 1)
                for j in range(KB):
                    pe.wait_ge(s_hid_hi, n * 8 - 3 + j)
                    last = product(ps_y[:], W3 + j * P, h3_hi[:, j, :], h3_lo[:, j, :], j == 0, j == KB - 1, exact,
                                   (s_hid_lo, n * 8 - 3 + j))
                last.then_inc(s_y, 1)

            def transpose_y(n):
                pe.wait_ge(s_y_t, n)
                transpose4(ps_y, lambda s: y_t[:, s * P:(s + 1) * P]).then_inc(s_yb, 1)

            def z_transpose(t):
                pe.wait_ge(s_z, t + 1)
                transpose4(ps_m, lambda s: z[:, s, :]).then_inc(s_zt, 1)

            def project(t):
                pe.wait_ge(s_zt_sb, t + 1)
                for b in range(SB):
                    last = nc.tensor.matmul(ps_m[:, 0:SEQ], wp_pad[:, b, :], z_t[:, b * SEQ:(b + 1) * SEQ],
                                            start=b == 0, stop=b == SB - 1)
                last.then_inc(s_xp, 1)

            def mix_out(t):
                pe.wait_ge(s_state, t + 1)
                dst = ps_m[:].rearrange("p (b h f) -> p b h f", b=SB, h=SUB // SB)
                for h in range(SUB // SB):
                    last = nc.tensor.matmul(dst[:, :, h, :], state[:, h * P:(h + 1) * P], cwo[:],
                                            start=h == 0, stop=h == SUB // SB - 1, skip_group_check=True)
                last.then_inc(s_mix, 1)

            def prepare(ph):
                kind, t = ph.prepare
                if ph.mix is not None:
                    pe.wait_ge(s_mixed, ph.mix + 1)
                if kind == "A":
                    transpose_input(ph.n + 1, xn_a, s_xn_a, t + 1)
                else:
                    transpose_input(ph.n + 1, xn_b, s_xn_b, t + 1)

            def phase(ph, exact):
                n = ph.n
                for k in range(KB):
                    if ph.start:
                        layer1(n, k, exact)
                    if ph.finish:
                        hidden(n * 8 - 4 + k, k, H2, h2_hi, h2_lo, (s_hid_hi, n * 8 - 8), (s_hid_lo, n * 8 - 8), exact)
                    if ph.mix is not None:
                        if k == 0:
                            z_transpose(ph.mix)
                        if k == 1:
                            project(ph.mix)
                        if k == 3:
                            mix_out(ph.mix)
                if ph.start:
                    for k in range(KB):
                        hidden(n * 8 + k, k, H1, h1_hi, h1_lo, (s_h1_hi, n * KB), (s_h1_lo, n * KB), exact)
                        if ph.finish and k == 1:
                            last_layer(n, exact)
                        if ph.finish and k == 2:
                            transpose_y(n)
                        if ph.prepare and k == (KB - 1 if ph.late else KB - 2):
                            prepare(ph)
                else:
                    last_layer(n, exact)
                    transpose_y(n)

            def all_phases(exact):
                for ph in HEAD:
                    phase(ph, exact)
                with pe.Fori(LOOP_FIRST, LOOP_END) as i:
                    for ph in loop_phases(i):
                        phase(ph, exact)
                for ph in TAIL:
                    phase(ph, exact)

            pe.wait_ge(s_ident, 1)
            transpose_input(0, xn_a, s_xn_a, 1)
            pe.wait_ge(s_pad, N_PAD)
            pe.wait_ge(s_par, N_PAR)
            nc.tensor.matmul(ps_y[0:SB * CH, 0:P], c_diag[:].rearrange("k b d -> k (b d)"), wo_in[:], start=True,
                             stop=True).then_inc(s_cwo, 1)
            pe.wait_ge(s_odd, 1)
            pe.wait_ge(s_cwo_sb, 1)
            nc.tensor.matmul(ps_y[0:1, 0:1], odd_col[:], ones_col[:], start=True, stop=True).then_inc(s_oddsum, 1)
            pe.wait_ge(s_flag, 1)
            odd = pe.value_load(odd_flag[0:1, 0:1])
            with pe.If(odd == 0):
                all_phases(exact=True)
            with pe.Else():
                pe.wait_ge(s_wlo, WCOLS // HID)
                all_phases(exact=False)


_OUT = ((P, NT, SUB, P), "float32")


def kernel(L0_attn_x, L0_attn_Wp, L0_attn_bp, L0_attn_Wo, L0_attn_bo, L0_attn_log_neg_lambdas, L0_attn_B_param,
           L0_attn_C_param, L0_attn_ln_gamma, L0_attn_ln_beta, L0_ffn_w1_w, L0_ffn_w1_s, L0_ffn_w2_w, L0_ffn_w2_s,
           L0_ffn_h1_w, L0_ffn_h1_s, L0_ffn_h2_w, L0_ffn_h2_s, L0_ffn_w3_w, L0_ffn_w3_s):
    import numpy as np
    import concourse.bacc as bacc
    from concourse.bass_utils import run_bass_kernel_spmd

    def blocks(w):
        w = np.asarray(w)
        o, i = w.shape
        return w.T.reshape(i // P, P, o).transpose(1, 0, 2).reshape(P, -1)

    def column(s):
        s = np.asarray(s).reshape(-1, P).T
        return np.concatenate([s, np.zeros((P, KB - s.shape[1]), s.dtype)], 1)

    arrays = {
        "x": np.asarray(L0_attn_x).reshape(NT, SUB, P, P).transpose(2, 0, 1, 3),
        "weights": np.concatenate([blocks(w) for w in (L0_ffn_w1_w, L0_ffn_w2_w, L0_ffn_h1_w, L0_ffn_h2_w,
                                                       L0_ffn_w3_w)], 1),
        "scales": np.stack([column(s) for s in (L0_ffn_w1_s, L0_ffn_w2_s, L0_ffn_h1_s, L0_ffn_h2_s,
                                                L0_ffn_w3_s)], 1),
        "rows": np.stack([np.asarray(v) for v in (L0_attn_bo, L0_attn_ln_gamma, L0_attn_ln_beta)]),
        "wp": np.asarray(L0_attn_Wp),
        "cmat": np.asarray(L0_attn_C_param),
        "wo": np.asarray(L0_attn_Wo),
        "chan": np.stack([np.asarray(v).reshape(-1) for v in (L0_attn_log_neg_lambdas, L0_attn_B_param,
                                                              L0_attn_bp)], 1),
    }
    nc = bacc.Bacc("TRN2", target_bir_lowering=False, num_devices=1)
    ins = {}
    aps = []
    for name, a in arrays.items():
        a = np.ascontiguousarray(a)
        ins[f"in_{name}"] = a
        aps.append(nc.dram_tensor(f"in_{name}", a.shape, mybir.dt.from_np(a.dtype), kind="ExternalInput").ap())
    out = nc.dram_tensor("out", _OUT[0], mybir.dt.from_np(np.dtype(_OUT[1])), kind="ExternalOutput").ap()
    macaron_kernel(nc, *aps, out)
    r = run_bass_kernel_spmd(nc, [ins], core_ids=[0])
    got = r.results[0]["out"]
    return got.transpose(1, 2, 0, 3).reshape(BATCH, SEQ, P)
```

```python
import concourse.bass as bass
from concourse import mybir
from contextlib import ExitStack

f32 = mybir.dt.float32
f32r = mybir.dt.float32r
u16 = mybir.dt.uint16
i32 = mybir.dt.int32
ALU = mybir.AluOpType
ACT = mybir.ActivationFunctionType
AX = mybir.AxisListType

P = 128
BATCH, SEQ = 16, 256
TOK = 512
NT = BATCH * SEQ // TOK
SUB = TOK // P
SB = TOK // SEQ
HID = 512
KB = HID // P
CH = 32
HEADS, DH = 2, 16
EPS = 1e-5
UNITS = 2 * NT

W1, W2 = 0, HID
H1, H2 = 2 * HID, 2 * HID + KB * HID
W3 = 2 * HID + 2 * KB * HID
WCOLS = W3 + KB * P
SECTIONS = [(W1, W2), (W2, H1), (H1, H2), (H2, W3), (W3, WCOLS)]

CHECKS = 2 + 2 + KB + 1


def b_unit(t):
    if isinstance(t, int) and t >= NT - 2:
        return UNITS - NT + t
    return t * 2 + 3


IDLE = 6
POOL_STEPS, DVE_STEPS = 14, 48


class Steps:

    def __init__(self, eng, sem):
        self.eng, self.sem, self.base, self.n = eng, sem, 0, 0

    def add(self, ins):
        self.n += 1
        ins.then_inc(self.sem, 1)
        return self.base + self.n

    def wait(self, value):
        self.eng.wait_ge(self.sem, value)

    def enter(self, i, first, per_turn):
        self.start, self.first, self.per_turn = self.base + self.n, first, per_turn
        self.base, self.n = (i - first) * per_turn + self.start, 0

    def leave(self, turns):
        assert self.n == self.per_turn, (self.n, self.per_turn)
        self.base, self.n = self.start + turns * self.per_turn, 0


class Phase:

    def __init__(self, n, start=True, finish=None, mix=None, prepare=None, norm=None, late=False):
        self.n, self.start, self.finish, self.mix, self.prepare = n, start, finish, mix, prepare
        self.norm, self.late = norm, late


HEAD = [
    Phase(0, prepare=("A", 1)),
    Phase(1, finish=("A", 0), prepare=("A", 2)),
    Phase(2, finish=("A", 1), mix=0, prepare=("B", 0), late=True),
    Phase(3, finish=("A", 2), mix=1, prepare=("A", 3), late=None),
]
LOOP_FIRST, LOOP_END = 2, NT - 2


def loop_phases(i):
    return [
        Phase(i * 2, finish=("B", i - 2), mix=i, prepare=("B", i - 1)),
        Phase(i * 2 + 1, finish=("A", i + 1), prepare=("A", i + 2), norm=i),
    ]


TAIL = [
    Phase(2 * NT - 4, finish=("B", NT - 4), mix=NT - 2, prepare=("B", NT - 3)),
    Phase(2 * NT - 3, finish=("A", NT - 1), prepare=("B", NT - 2), norm=NT - 2),
    Phase(2 * NT - 2, finish=("B", NT - 3), mix=NT - 1, prepare=("B", NT - 1), late=True),
    Phase(2 * NT - 1, finish=("B", NT - 2)),
    Phase(2 * NT, start=False, finish=("B", NT - 1)),
]


def tile_of(a, t):
    return a[:, t] if isinstance(t, int) else a[:, bass.ds(t, 1)].rearrange("p o s f -> p (o s) f")


def above(value, least):
    return not isinstance(value, int) or value >= least


def macaron_kernel(nc, x, weights, scales, rows, wp, cmat, wo, chan, out):
    ctx = ExitStack()
    with ctx:
        def sb(name, shape, dt=f32):
            return ctx.enter_context(nc.sbuf_tensor(name, shape, dt))

        def pb(name):
            return ctx.enter_context(nc.psum_tensor(name, [P, TOK], f32))

        def sem(name):
            return ctx.enter_context(nc.semaphore(name))

        w_raw = sb("w_raw", [P, WCOLS])
        w_hi = sb("w_hi", [P, WCOLS], f32r)
        w_lo = sb("w_lo", [P, WCOLS], f32r)
        low_half = sb("low_half", [P, 2 * HID], mybir.dt.bfloat16)
        odd_cols = sb("odd_cols", [P, CHECKS])
        odd_flag = sb("odd_flag", [1, 1], i32)
        ones_col = sb("ones_col", [P, 1])
        scale_in = sb("scale_in", [P, 5, KB])
        half_s1 = sb("half_s1", [P, KB])
        gate_s = sb("gate_s", [P, KB])
        half_s3 = sb("half_s3", [P, 1])
        row_in = sb("row_in", [P, 3, P])
        bo_bc, gamma_bc, beta_bc = (row_in[:, r, :] for r in range(3))
        bo4 = sb("bo4", [P, SUB, P])
        beta4 = sb("beta4", [P, SUB, P])
        ident = sb("ident", [P, P])
        wp_pad = sb("wp_pad", [P, SB, P])
        c_diag = sb("c_diag", [CH, SB, CH])
        wo_in = sb("wo_in", [CH, P])
        cwo = sb("cwo", [P, SB, P])
        chan_in = sb("chan_in", [SB * CH, 3])
        lam_t = sb("lam_t", [SB * CH, 1])
        lam = sb("lam", [SB * CH, SEQ])
        act_idle = sb("act_idle", [P, 1])
        pool_idle, dve_idle = sb("pool_idle", [P, IDLE]), sb("dve_idle", [P, IDLE])
        minus_half = sb("minus_half", [P, SUB])

        x_all = sb("x_all", [P, NT, SUB, P])
        x2_all = sb("x2_all", [P, NT, SUB, P])
        x1 = sb("x1", [P, SUB, P])
        x2 = sb("x2", [P, SUB, P])
        xn_a = sb("xn_a", [P, SUB, P])
        xn_b = sb("xn_b", [P, SUB, P])
        z = sb("z", [P, SUB, P])
        z_bo = sb("z_bo", [P, SUB, P])
        x1_beta = sb("x1_beta", [P, SUB, P])
        mixed = sb("mixed", [P, SUB, P])
        centred = sb("centred", [P, SUB, P])
        out_sb = sb("out_sb", [P, SUB, P])
        ln = {k: dict(stats=sb(f"stats_{k}", [P, SUB, 6]), mv=sb(f"mv_{k}", [P, SUB, 2]),
                      var=sb(f"var_{k}", [P, SUB]), neg=sb(f"neg_{k}", [P, SUB]), rstd=sb(f"rstd_{k}", [P, SUB])) for k in ("a", "z", "mix", "b")}
        xt_hi = sb("xt_hi", [P, TOK], f32r)
        xt_lo = sb("xt_lo", [P, TOK], f32r)
        z_t = sb("z_t", [P, TOK])
        tanh_g = sb("tanh_g", [P, 2, TOK])
        gate = sb("gate", [P, 2, TOK])
        h1f = sb("h1f", [P, 2, TOK])
        h1_hi = sb("h1_hi", [P, KB, TOK], f32r)
        h1_lo = sb("h1_lo", [P, KB, TOK], f32r)
        hf = sb("hf", [P, 2, TOK])
        h2_hi = sb("h2_hi", [P, KB, TOK], f32r)
        h2_lo = sb("h2_lo", [P, KB, TOK], f32r)
        h3_hi = sb("h3_hi", [P, KB, TOK], f32r)
        h3_lo = sb("h3_lo", [P, KB, TOK], f32r)
        y_t = sb("y_t", [P, TOK])
        u_in = sb("u_in", [SB * CH, SEQ])
        state = sb("state", [P, SEQ])

        ps_g = [pb(f"ps_g{j}") for j in range(2)]
        ps_u = [pb(f"ps_u{j}") for j in range(2)]
        ps_h = [pb(f"ps_h{j}") for j in range(2)]
        ps_y = pb("ps_y")
        ps_m = pb("ps_m")

        s_x = [sem(f"x_loaded{t}") for t in range(2)]
        s_xrest = sem("x_rest_loaded")
        s_w = [sem(f"weights_loaded{j}") for j in range(len(SECTIONS))]
        s_scale = sem("scales_loaded")
        s_chan = sem("channels_loaded")
        s_par = sem("params_loaded")
        s_zero = sem("zeros_written")
        s_pad = sem("padded_loaded")
        s_ident = sem("ident_ready")
        s_const = sem("dve_consts_ready")
        s_whi = sem("w_hi_ready")
        s_check = sem("weights_checked")
        s_ones = sem("ones_ready")
        s_wlo = sem("w_lo_ready")
        s_oddsum = sem("odd_sum_ready")
        s_flag = sem("flag_ready")
        s_half = sem("half_scales_ready")
        s_cwo_sb = sem("cwo_ready")
        s_cwo = sem("cwo_product_ready")
        s_lam = sem("lam_tanh_ready")
        s_xn_a = sem("xn_a_ready")
        s_xn_b = sem("xn_b_ready")
        s_xt = sem("xt_transposed")
        s_xt_hi = sem("xt_hi_ready")
        s_xt_lo = sem("xt_lo_ready")
        s_l1 = sem("l1_done")
        s_tanh = sem("tanh_ready")
        s_h1f = sem("h1f_ready")
        s_h1_hi = sem("h1_hi_ready")
        s_h1_lo = sem("h1_lo_ready")
        s_hid = sem("hidden_done")
        s_hid_hi = sem("hidden_hi_ready")
        s_hid_f = sem("hidden_full_ready")
        s_hid_lo = sem("hidden_lo_ready")
        s_y = sem("y_done")
        s_y_t = sem("y_scaled")
        s_yb = sem("y_transposed")
        s_fin = sem("y_added")
        s_z_st = sem("z_stats_ready")
        s_z = sem("z_ready")
        s_zbo = sem("z_bo_ready")
        s_x1b = sem("x1_beta_ready")
        s_zt = sem("z_transposed")
        s_zt_sb = sem("z_t_ready")
        s_xp = sem("xp_done")
        s_state = sem("state_ready")
        s_mix = sem("mix_product_done")
        s_mixed = sem("mixed_ready")
        s_mix_st = sem("mix_stats_ready")
        s_mix_r = sem("mix_rstd_ready")
        s_x2 = sem("x2_ready")
        s_b_st = sem("b_stats_ready")
        s_a_st = sem("a_stats_ready")
        s_a_r = sem("a_rstd_ready")
        s_stored = sem("out_stored")
        s_dve = sem("dve_steps")
        s_pool = sem("pool_steps")

        block = ctx.enter_context(nc.Block())

        @block.sync
        def _(sp):
            sp.dma_start(x_all[:, 0], x[:, 0]).then_inc(s_x[0], 16)
            for j, (a, b) in enumerate(SECTIONS):
                sp.dma_start(w_raw[:, a:b], weights[:, a:b]).then_inc(s_w[j], 16)
                if j == 2:
                    sp.dma_start(x_all[:, 1], x[:, 1]).then_inc(s_x[1], 16)
            for r in range(3):
                sp.dma_start(row_in[:, r, :], rows[r:r + 1, :].to_broadcast([P, P])).then_inc(s_par, 16)
            sp.dma_start(wo_in[:], wo).then_inc(s_par, 16)
            sp.wait_ge(s_zero, 3)
            for b in range(SB):
                sp.dma_start(wp_pad[:, b, CH * b:CH * b + CH], wp).then_inc(s_pad, 16)
                for h in range(HEADS):
                    sp.dma_start(c_diag[DH * h:DH * h + DH, b, DH * h:DH * h + DH], cmat[h]).then_inc(s_pad, 16)
            sp.dma_start(x_all[:, 2:NT], x[:, 2:NT]).then_inc(s_xrest, 16)

            def store(t):
                sp.wait_ge(s_fin, b_unit(t) + 1)
                sp.dma_start(tile_of(out, t), out_sb[:]).then_inc(s_stored, 16)

            with sp.Fori(0, NT - 2) as t:
                store(t)
            store(NT - 2)
            store(NT - 1)
            sp.wait_ge(s_stored, 16 * NT)

        N_PAR = 16 * (3 + 1)
        N_PAD = 16 * SB * (1 + HEADS)

        @block.gpsimd
        def _(pool):
            st = Steps(pool, s_pool)
            nc.gpsimd.memset(minus_half[:], -0.5).then_inc(s_zero, 1)
            v = st.add(nc.gpsimd.memset(ident[:], 0.0))
            nc.gpsimd.memset(wp_pad[:], 0.0).then_inc(s_zero, 1)
            nc.gpsimd.memset(c_diag[:], 0.0).then_inc(s_zero, 1)
            st.wait(v)
            nc.gpsimd.affine_select(out=ident[:], in_=ident[:], compare_op=ALU.not_equal, fill=1.0, base=0,
                                    pattern=[[-1, P]], channel_multiplier=1).then_inc(s_ident, 1)


            idle = [0]

            def wait_alone(semaphore, value):
                pool.wait_ge(semaphore, value)
                if not isinstance(value, int):
                    idle[0] = (idle[0] + 1) % IDLE
                    nc.gpsimd.tensor_tensor(pool_idle[:, idle[0]:idle[0] + 1], minus_half[:, 0:1],
                                            minus_half[:, 1:2], ALU.add)


            def rstd(kind):
                c = ln[kind]
                v = st.add(nc.gpsimd.tensor_scalar(c["var"][:], c["mv"][:, :, 1], EPS, None, ALU.add))
                st.wait(v)
                return nc.gpsimd.tensor_tensor(c["rstd"][:], c["var"][:], minus_half[:], ALU.pow)

            def negate_mean(kind):
                c = ln[kind]
                return nc.gpsimd.tensor_scalar(c["neg"][:], c["mv"][:, :, 0], -1.0, None, ALU.mult)

            def normalise(kind, dst, src):
                c = ln[kind]
                for s in range(SUB):
                    last = nc.gpsimd.tensor_scalar(dst[:, s, :], src[:, s, :], c["neg"][:, s:s + 1],
                                                   c["rstd"][:, s:s + 1], ALU.add, ALU.mult)
                    if s < SUB - 1:
                        st.add(last)
                return last

            def rstd_a(count):
                wait_alone(s_a_st, count)
                rstd("a").then_inc(s_a_r, 1)

            def w_to_lo(sections):
                for j in sections:
                    pool.wait_ge(s_whi, j + 1)
                    for c in range(*SECTIONS[j], HID):
                        nc.gpsimd.tensor_tensor(w_lo[:, c:c + HID], w_raw[:, c:c + HID],
                                                w_hi[:, c:c + HID].bitcast(f32), ALU.subtract).then_inc(s_wlo, 1)

            def phase(ph):
                n = ph.n
                for k in range(KB):
                    if ph.start:
                        pool.wait_ge(s_h1_hi, n * KB + k + 1)
                        if k == 0 and above(n, 1):
                            pool.wait_ge(s_hid, n * 8 - 4)
                        nc.gpsimd.tensor_tensor(h1_lo[:, k, :], h1f[:, k % 2, :], h1_hi[:, k, :].bitcast(f32),
                                                ALU.subtract).then_inc(s_h1_lo, 1)
                    if k == 1 and ph.prepare and ph.prepare[0] == "A":
                        rstd_a(ph.prepare[1] + 1)
                    if k == 2 and ph.mix is not None:
                        residuals(ph.mix)
                if isinstance(n, int) and n == 0:
                    pool.wait_ge(s_flag, 1)
                    odd = pool.value_load(odd_flag[0:1, 0:1])
                    with pool.If(odd != 0):
                        w_to_lo(range(2, len(SECTIONS)))
                if ph.norm is not None:
                    normalise_b(ph.norm)
                if ph.mix is not None:
                    wait_alone(s_mix_st, ph.mix + 1)
                    rstd("mix").then_inc(s_mix_r, 1)
                    if ph.late is not False:
                        normalise_b(ph.mix)
                if ph.finish and ph.finish[0] == "A":
                    t = ph.finish[1]
                    if above(t, 1):
                        pool.wait_ge(s_zt, t)
                    wait_alone(s_z_st, t + 1)
                    st.add(negate_mean("z"))
                    v = st.add(rstd("z"))
                    wait_alone(st.sem, v)
                    normalise("z", z, x1[:]).then_inc(s_z, 1)

            def normalise_b(t):
                if above(t, 1):
                    pool.wait_ge(s_xt, b_unit(t - 1) + 1)
                wait_alone(s_b_st, t + 1)
                st.add(negate_mean("b"))
                v = st.add(rstd("b"))
                wait_alone(st.sem, v)
                normalise("b", xn_b, x2).then_inc(s_xn_b, 1)

            def residuals(t):
                pool.wait_ge(s_z, t + 1)
                if isinstance(t, int) and t == 0:
                    pool.wait_ge(s_const, 1)
                if above(t, 1):
                    pool.wait_ge(s_x2, t)
                nc.gpsimd.tensor_tensor(z_bo[:], z[:], bo4[:], ALU.add).then_inc(s_zbo, 1)
                nc.gpsimd.tensor_tensor(x1_beta[:], x1[:], beta4[:], ALU.add).then_inc(s_x1b, 1)

            rstd_a(1)
            w_to_lo(range(0, 2))

            for ph in HEAD:
                phase(ph)
            with pool.Fori(LOOP_FIRST, LOOP_END) as i:
                st.enter(i, LOOP_FIRST, POOL_STEPS)
                for ph in loop_phases(i):
                    phase(ph)
                st.leave(LOOP_END - LOOP_FIRST)
            for ph in TAIL:
                phase(ph)

        @block.scalar
        def _(act):
            act.dma_start(scale_in[:], scales).then_inc(s_scale, 16)
            for b in range(SB):
                act.dma_start(chan_in[CH * b:CH * b + CH, :], chan).then_inc(s_chan, 16)
            act.wait_ge(s_zero, 1)
            nc.scalar.activation(act_idle[:], minus_half[:, 0:1], ACT.Gelu).then_inc(s_lam, 1)

            def xt_to_hi(n):
                act.wait_ge(s_xt, n + 1)
                nc.scalar.activation(xt_hi[:], ps_m[:], ACT.Copy).then_inc(s_xt_hi, 1)

            def gelu(q, k, scale, dst_hi):
                act.wait_ge(s_hid, q + 1)
                nc.scalar.activation(dst_hi, ps_h[k % 2][:], ACT.Gelu, scale=scale).then_inc(s_hid_hi, 1)
                if above(q, 2):
                    act.wait_ge(s_hid_lo, q - 1)
                nc.scalar.activation(hf[:, k % 2, :], ps_h[k % 2][:], ACT.Gelu, scale=scale).then_inc(s_hid_f, 1)

            def tanh(n, k):
                q = n * KB + k
                act.wait_ge(s_l1, q + 1)
                if above(q, 2):
                    act.wait_ge(s_h1f, q - 1)
                nc.scalar.activation(tanh_g[:, k % 2, :], ps_g[k % 2][:], ACT.Tanh,
                                     scale=half_s1[:, k:k + 1]).then_inc(s_tanh, 1)

            def round_h1(n, k):
                act.wait_ge(s_h1f, n * KB + k + 1)
                nc.scalar.activation(h1_hi[:, k, :], h1f[:, k % 2, :], ACT.Copy).then_inc(s_h1_hi, 1)

            def gelu3(n, k):
                gelu(n * 8 - 4 + k, k, scale_in[:, 3, k:k + 1], h3_hi[:, k, :])

            def phase(ph):
                n = ph.n
                if ph.start and ph.finish:
                    tanh(n, 0)
                    tanh(n, 1)
                    round_h1(n, 0)
                    gelu3(n, 0)
                    round_h1(n, 1)
                    if ph.mix is not None:
                        act.wait_ge(s_zt, ph.mix + 1)
                        nc.scalar.activation(z_t[:], ps_m[:], ACT.Copy).then_inc(s_zt_sb, 1)
                    tanh(n, 2)
                    gelu3(n, 1)
                    tanh(n, 3)
                    round_h1(n, 2)
                    round_h1(n, 3)
                    gelu3(n, 2)
                    gelu3(n, 3)
                elif ph.start:
                    tanh(n, 0)
                    tanh(n, 1)
                    for k in range(KB):
                        round_h1(n, k)
                        check_weights(H2 + k * HID, H2 + (k + 1) * HID, 3)
                        if k < 2:
                            tanh(n, k + 2)
                    check_weights(W3, WCOLS, 4)
                else:
                    for k in range(KB):
                        gelu3(n, k)
                if ph.start:
                    for k in range(KB):
                        gelu(n * 8 + k, k, scale_in[:, 2, k:k + 1], h2_hi[:, k, :])
                        if k == 1 and ph.finish:
                            scale_y(n)
                        if k == (KB - 1 if ph.late else 1) and ph.prepare:
                            xt_to_hi(n + 1)
                else:
                    scale_y(n)

            def scale_y(n):
                act.wait_ge(s_y, n)
                nc.scalar.activation(y_t[:], ps_y[:], ACT.Copy, scale=half_s3[:]).then_inc(s_y_t, 1)

            def check_weights(a, b, section):
                act.wait_ge(s_w[section], 16)
                low = w_raw[:, a:b].bitcast(u16).rearrange("p (n two) -> p n two", two=2)[:, :, 0]
                at = checks[0]
                checks[0] += 1
                nc.scalar.activation(low_half[:, 0:b - a], low, ACT.Copy,
                                     accum_out=odd_cols[:, at:at + 1]).then_inc(s_check, 1)
                act.wait_ge(s_check, at + 1)

            checks = [0]
            check_weights(W1, W2, 0)
            check_weights(W2, H1, 1)
            act.wait_ge(s_chan, 16 * SB)
            nc.scalar.activation(lam_t[:], chan_in[:, 0:1], ACT.Tanh, scale=0.5).then_inc(s_lam, 1)
            xt_to_hi(0)
            for c in range(H1, H2, 2 * HID):
                check_weights(c, c + 2 * HID, 2)
            act.wait_ge(s_half, 1)
            for ph in HEAD:
                phase(ph)
            with act.Fori(LOOP_FIRST, LOOP_END) as i:
                for ph in loop_phases(i):
                    phase(ph)
            for ph in TAIL:
                phase(ph)

        @block.vector
        def _(dve):
            st = Steps(dve, s_dve)

            idle = [0]

            def wait_alone(semaphore, value):
                dve.wait_ge(semaphore, value)
                if not isinstance(value, int):
                    idle[0] = (idle[0] + 1) % IDLE
                    nc.vector.memset(dve_idle[:, idle[0]:idle[0] + 1], 0.0)


            def layer_stats(kind, src, first_wait=None):
                for s in range(SUB):
                    v = st.add(nc.vector.bn_stats(ln[kind]["stats"][:, s, :], src(s)))
                wait_alone(st.sem, v)
                for s in range(SUB):
                    last = nc.vector.bn_aggr(ln[kind]["mv"][:, s, :], ln[kind]["stats"][:, s, :])
                    if s < SUB - 1:
                        st.add(last)
                return last

            def stats_a(t):
                src = tile_of(x_all, t)
                layer_stats("a", lambda s: src[:, s, :]).then_inc(s_a_st, 1)

            def normalise_a(t):
                dve.wait_ge(s_a_r, t + 1)
                dve.wait_ge(s_a_st, t + 1)
                src = tile_of(x_all, t)
                for s in range(SUB):
                    last = nc.vector.tensor_scalar(xn_a[:, s, :], src[:, s, :], ln["a"]["mv"][:, s, 0:1],
                                                   ln["a"]["rstd"][:, s:s + 1], ALU.subtract, ALU.mult)
                    if s < SUB - 1:
                        st.add(last)
                last.then_inc(s_xn_a, 1)

            def xt_to_lo(n):
                dve.wait_ge(s_xt_hi, n + 1)
                nc.vector.tensor_tensor(xt_lo[:], ps_m[:], xt_hi[:].bitcast(f32), ALU.subtract).then_inc(s_xt_lo, 1)

            def hidden_lo(q, k, hi, lo):
                dve.wait_ge(s_hid_f, q + 1)
                nc.vector.tensor_tensor(lo, hf[:, k % 2, :], hi.bitcast(f32), ALU.subtract).then_inc(s_hid_lo, 1)

            def recur(t):
                dve.wait_ge(s_xp, t + 1)
                v = st.add(nc.vector.tensor_scalar(u_in[:], ps_m[0:SB * CH, 0:SEQ], chan_in[:, 2:3], chan_in[:, 1:2],
                                                   ALU.add, ALU.mult))
                st.wait(v)
                nc.vector.tensor_tensor_scan(state[0:SB * CH, :], lam[:], u_in[:], 0.0, ALU.mult,
                                             ALU.add).then_inc(s_state, 1)

            def mixer_sum(t):
                dve.wait_ge(s_mix, t + 1)
                dve.wait_ge(s_zbo, t + 1)
                nc.vector.tensor_tensor(mixed[:], ps_m[:].rearrange("p (s f) -> p s f", s=SUB), z_bo[:],
                                        ALU.add).then_inc(s_mixed, 1)
                dve.wait_ge(s_mixed, t + 1)
                layer_stats("mix", lambda s: mixed[:, s, :]).then_inc(s_mix_st, 1)

            def mixer_norm(t):
                dve.wait_ge(s_mix_r, t + 1)
                dve.wait_ge(s_mix_st, t + 1)
                for s in range(SUB):
                    v = st.add(nc.vector.scalar_tensor_tensor(
                        out=centred[:, s, :], in0=mixed[:, s, :], scalar=ln["mix"]["mv"][:, s, 0:1], in1=gamma_bc,
                        op0=ALU.subtract, op1=ALU.mult))
                dve.wait_ge(s_x1b, t + 1)
                st.wait(v)
                if above(t, 1):
                    dve.wait_ge(s_xn_b, t)
                for s in range(SUB):
                    last = nc.vector.scalar_tensor_tensor(
                        out=x2[:, s, :], in0=centred[:, s, :], scalar=ln["mix"]["rstd"][:, s:s + 1],
                        in1=x1_beta[:, s, :], op0=ALU.mult, op1=ALU.add)
                    if s < SUB - 1:
                        st.add(last)
                last.then_inc(s_x2, 1)

            def b_stats(t):
                dve.wait_ge(s_x2, t + 1)
                layer_stats("b", lambda s: x2[:, s, :]).then_inc(s_b_st, 1)
                st.add(nc.vector.tensor_copy(tile_of(x2_all, t), x2[:]))

            def finish(kind, t, n):
                dve.wait_ge(s_yb, n)
                y = ps_y[:].rearrange("p (s f) -> p s f", s=SUB)
                if kind == "A":
                    if above(t, 1):
                        dve.wait_ge(s_x1b, t)
                    nc.vector.tensor_tensor(x1[:], y, tile_of(x_all, t), ALU.add).then_inc(s_fin, 1)
                else:
                    if above(t, 1):
                        dve.wait_ge(s_stored, t * 16)
                    nc.vector.tensor_tensor(out_sb[:], y, tile_of(x2_all, t), ALU.add).then_inc(s_fin, 1)

            def finish_stats(n):
                dve.wait_ge(s_fin, n)
                layer_stats("z", lambda s: x1[:, s, :]).then_inc(s_z_st, 1)

            def gated(n, k):
                q = n * KB + k
                dve.wait_ge(s_tanh, q + 1)
                v = st.add(nc.vector.scalar_tensor_tensor(
                    out=gate[:, k % 2, :], in0=tanh_g[:, k % 2, :], scalar=1.0, in1=ps_g[k % 2][:],
                    op0=ALU.add, op1=ALU.mult))
                st.wait(v)
                if above(q, 2):
                    dve.wait_ge(s_h1_hi, q - 1)
                    dve.wait_ge(s_h1_lo, q - 1)
                nc.vector.scalar_tensor_tensor(
                    out=h1f[:, k % 2, :], in0=ps_u[k % 2][:], scalar=gate_s[:, k:k + 1], in1=gate[:, k % 2, :],
                    op0=ALU.mult, op1=ALU.mult).then_inc(s_h1f, 1)

            def lo3(n, k):
                hidden_lo(n * 8 - 4 + k, k, h3_hi[:, k, :], h3_lo[:, k, :])

            def lo2(n, k):
                hidden_lo(n * 8 + k, k, h2_hi[:, k, :], h2_lo[:, k, :])

            def round_weights(a, b, section):
                dve.wait_ge(s_w[section], 16)
                return nc.vector.tensor_copy(w_hi[:, a:b], w_raw[:, a:b])

            def phase(ph):
                n = ph.n
                prepare_a = ph.prepare[1] if ph.prepare and ph.prepare[0] == "A" else None

                def stats_next_a():
                    if not isinstance(prepare_a, int) or prepare_a >= 2:
                        dve.wait_ge(s_xrest, 16)
                    else:
                        dve.wait_ge(s_x[prepare_a], 16)
                    stats_a(prepare_a)

                if ph.start and ph.finish:
                    gated(n, 0)
                    gated(n, 1)
                    lo3(n, 0)
                    if prepare_a is not None:
                        stats_next_a()
                    gated(n, 2)
                    gated(n, 3)
                    lo3(n, 1)
                    if ph.mix is not None:
                        recur(ph.mix)
                    lo3(n, 2)
                    if prepare_a is not None:
                        normalise_a(prepare_a)
                    if ph.mix is not None:
                        mixer_sum(ph.mix)
                    lo3(n, 3)
                    if ph.norm is not None:
                        b_stats(ph.norm)
                elif ph.start:
                    gated(n, 0)
                    stats_next_a()
                    gated(n, 1)
                    st.add(round_weights(H2, H2 + 2 * HID, 3))
                    gated(n, 2)
                    gated(n, 3)
                    normalise_a(prepare_a)
                    round_weights(H2 + 2 * HID, W3, 3).then_inc(s_whi, 1)
                    round_weights(W3, WCOLS, 4).then_inc(s_whi, 1)
                    dve.wait_ge(s_par, N_PAR)
                    st.add(nc.vector.tensor_copy(bo4[:], bo_bc.unsqueeze(1).broadcast_to([P, SUB, P])))
                    nc.vector.tensor_copy(beta4[:], beta_bc.unsqueeze(1).broadcast_to([P, SUB, P])).then_inc(s_const, 1)
                    dve.wait_ge(s_cwo, 1)
                    for b in range(SB):
                        rows_b = slice(CH * b, CH * b + CH)
                        last = nc.vector.tensor_copy(cwo[rows_b, b, :], ps_y[rows_b, 0:P])
                        if b < SB - 1:
                            st.add(last)
                    last.then_inc(s_cwo_sb, 1)
                    dve.wait_ge(s_oddsum, 1)
                    nc.vector.tensor_reduce(odd_flag[:], ps_y[0:1, 0:CHECKS], AX.X, ALU.max).then_inc(s_flag, 1)
                else:
                    for k in range(KB):
                        lo3(n, k)
                if ph.start:
                    lo2(n, 0)
                    if ph.mix is not None:
                        mixer_norm(ph.mix)
                        if ph.late:
                            b_stats(ph.mix)
                    lo2(n, 1)
                    if ph.prepare and not ph.late:
                        xt_to_lo(n + 1)
                    if ph.finish and ph.finish[0] == "A":
                        finish(*ph.finish, n)
                        finish_stats(n)
                        lo2(n, 2)
                    else:
                        lo2(n, 2)
                        if ph.finish:
                            finish(*ph.finish, n)
                    lo2(n, 3)
                    if ph.late is None:
                        b_stats(ph.mix)
                    if ph.late:
                        xt_to_lo(n + 1)
                else:
                    finish(*ph.finish, n)

            st.add(nc.vector.memset(ones_col[:], 1.0))
            st.add(nc.vector.memset(state[:], 0.0))
            st.add(nc.vector.memset(cwo[:], 0.0))
            nc.vector.memset(lam[:], 1.0).then_inc(s_ones, 1)
            dve.wait_ge(s_scale, 16)
            v = st.add(nc.vector.tensor_scalar(half_s1[:], scale_in[:, 0, :], 0.5, None, ALU.mult))
            nc.vector.tensor_scalar(half_s3[:], scale_in[:, 4, 0:1], 0.5, None, ALU.mult).then_inc(s_half, 1)
            st.wait(v)
            st.add(nc.vector.tensor_tensor(gate_s[:], half_s1[:], scale_in[:, 1, :], ALU.mult))
            dve.wait_ge(s_x[0], 16)
            stats_a(0)
            round_weights(W1, W2, 0).then_inc(s_whi, 1)
            round_weights(W2, H1, 1).then_inc(s_whi, 1)
            normalise_a(0)
            xt_to_lo(0)
            round_weights(H1, H2, 2).then_inc(s_whi, 1)
            dve.wait_ge(s_lam, 2)
            v = st.add(nc.vector.tensor_scalar(lam_t[:], lam_t[:], 0.5, 0.5, ALU.mult, ALU.add))
            st.wait(v)
            st.add(nc.vector.tensor_scalar(lam[:], lam[:], lam_t[:], None, ALU.mult))

            for ph in HEAD:
                phase(ph)
            with dve.Fori(LOOP_FIRST, LOOP_END) as i:
                st.enter(i, LOOP_FIRST, DVE_STEPS)
                for ph in loop_phases(i):
                    phase(ph)
                st.leave(LOOP_END - LOOP_FIRST)
            for ph in TAIL:
                phase(ph)

        @block.tensor
        def _(pe):
            def transpose4(dst, src):
                for s in range(SUB):
                    last = nc.tensor.transpose(dst[:, s * P:(s + 1) * P], src(s), ident[:])
                return last

            def product(dst, wcol, hi, lo, first, final, exact, lo_wait=None):
                w = w_hi[:, wcol:wcol + P]
                nc.tensor.matmul(dst, w, hi, start=first, stop=False)
                if not exact:
                    nc.tensor.matmul(dst, w_lo[:, wcol:wcol + P], hi, start=False, stop=False)
                if lo_wait:
                    pe.wait_ge(*lo_wait)
                last = nc.tensor.matmul(dst, w, lo, start=False, stop=final and exact)
                if not exact:
                    last = nc.tensor.matmul(dst, w_lo[:, wcol:wcol + P], lo, start=False, stop=final)
                return last

            def transpose_input(n, src, ready, count):
                pe.wait_ge(ready, count)
                transpose4(ps_m, lambda s: src[:, s, :]).then_inc(s_xt, 1)

            def layer1(n, k, exact):
                q = n * KB + k
                if k == 0:
                    pe.wait_ge(s_xt_hi, n + 1)
                if above(q, 2):
                    pe.wait_ge(s_h1f, q - 1)
                product(ps_g[k % 2][:], W1 + k * P, xt_hi[:], xt_lo[:], True, True, exact,
                        (s_xt_lo, n + 1) if k == 0 else None)
                product(ps_u[k % 2][:], W2 + k * P, xt_hi[:], xt_lo[:], True, True, exact).then_inc(s_l1, 1)

            def hidden(q, k, w0, hi, lo, hi_at, lo_at, exact):
                if above(q, 2):
                    pe.wait_ge(s_hid_f, q - 1)
                for j in range(KB):
                    if k == 0:
                        pe.wait_ge(hi_at[0], hi_at[1] + j + 1)
                    last = product(ps_h[k % 2][:], w0 + j * HID + k * P, hi[:, j, :], lo[:, j, :],
                                   j == 0, j == KB - 1, exact,
                                   (lo_at[0], lo_at[1] + j + 1) if k == 0 else None)
                last.then_inc(s_hid, 1)

            def last_layer(n, exact):
                if above(n, 2):
                    pe.wait_ge(s_fin, n - 1)
                for j in range(KB):
                    pe.wait_ge(s_hid_hi, n * 8 - 3 + j)
                    last = product(ps_y[:], W3 + j * P, h3_hi[:, j, :], h3_lo[:, j, :], j == 0, j == KB - 1, exact,
                                   (s_hid_lo, n * 8 - 3 + j))
                last.then_inc(s_y, 1)

            def transpose_y(n):
                pe.wait_ge(s_y_t, n)
                transpose4(ps_y, lambda s: y_t[:, s * P:(s + 1) * P]).then_inc(s_yb, 1)

            def z_transpose(t):
                pe.wait_ge(s_z, t + 1)
                transpose4(ps_m, lambda s: z[:, s, :]).then_inc(s_zt, 1)

            def project(t):
                pe.wait_ge(s_zt_sb, t + 1)
                for b in range(SB):
                    last = nc.tensor.matmul(ps_m[:, 0:SEQ], wp_pad[:, b, :], z_t[:, b * SEQ:(b + 1) * SEQ],
                                            start=b == 0, stop=b == SB - 1)
                last.then_inc(s_xp, 1)

            def mix_out(t):
                pe.wait_ge(s_state, t + 1)
                dst = ps_m[:].rearrange("p (b h f) -> p b h f", b=SB, h=SUB // SB)
                for h in range(SUB // SB):
                    last = nc.tensor.matmul(dst[:, :, h, :], state[:, h * P:(h + 1) * P], cwo[:],
                                            start=h == 0, stop=h == SUB // SB - 1, skip_group_check=True)
                last.then_inc(s_mix, 1)

            def prepare(ph):
                kind, t = ph.prepare
                if ph.mix is not None:
                    pe.wait_ge(s_mixed, ph.mix + 1)
                if kind == "A":
                    transpose_input(ph.n + 1, xn_a, s_xn_a, t + 1)
                else:
                    transpose_input(ph.n + 1, xn_b, s_xn_b, t + 1)

            def layer3(n, k, exact):
                hidden(n * 8 - 4 + k, k, H2, h2_hi, h2_lo, (s_hid_hi, n * 8 - 8), (s_hid_lo, n * 8 - 8), exact)

            def first_half(ph, exact):
                n = ph.n
                if ph.start and ph.finish:
                    layer1(n, 0, exact)
                    layer1(n, 1, exact)
                    layer3(n, 0, exact)
                    layer1(n, 2, exact)
                    if ph.mix is not None:
                        z_transpose(ph.mix)
                    layer3(n, 1, exact)
                    layer1(n, 3, exact)
                    layer3(n, 2, exact)
                    if ph.mix is not None:
                        project(ph.mix)
                    layer3(n, 3, exact)
                    if ph.mix is not None:
                        mix_out(ph.mix)
                else:
                    for k in range(KB):
                        if ph.start:
                            layer1(n, k, exact)
                        else:
                            layer3(n, k, exact)

            def second_half(ph, exact):
                n = ph.n
                if not ph.start:
                    last_layer(n, exact)
                    transpose_y(n)
                    return
                for k in range(KB):
                    hidden(n * 8 + k, k, H1, h1_hi, h1_lo, (s_h1_hi, n * KB), (s_h1_lo, n * KB), exact)
                    if k == 1 and ph.finish:
                        last_layer(n, exact)
                    if ph.prepare and k == (KB - 1 if ph.late else 1):
                        prepare(ph)
                    if k == 2 and ph.finish:
                        transpose_y(n)

            def phase(ph, exact):
                first_half(ph, exact)
                second_half(ph, exact)

            def all_phases(exact):
                second_half(HEAD[0], exact)
                for ph in HEAD[1:]:
                    phase(ph, exact)
                with pe.Fori(LOOP_FIRST, LOOP_END) as i:
                    for ph in loop_phases(i):
                        phase(ph, exact)
                for ph in TAIL:
                    phase(ph, exact)

            pe.wait_ge(s_ident, 1)
            transpose_input(0, xn_a, s_xn_a, 1)
            pe.wait_ge(s_whi, 2)
            pe.wait_ge(s_wlo, 2)
            first_half(HEAD[0], exact=False)
            pe.wait_ge(s_pad, N_PAD)
            pe.wait_ge(s_par, N_PAR)
            nc.tensor.matmul(ps_y[0:SB * CH, 0:P], c_diag[:].rearrange("k b d -> k (b d)"), wo_in[:], start=True,
                             stop=True).then_inc(s_cwo, 1)
            pe.wait_ge(s_cwo_sb, 1)
            pe.wait_ge(s_ones, 1)
            pe.wait_ge(s_check, CHECKS)
            nc.tensor.matmul(ps_y[0:1, 0:CHECKS], ones_col[:], odd_cols[:], start=True, stop=True).then_inc(s_oddsum, 1)
            pe.wait_ge(s_flag, 1)
            pe.wait_ge(s_whi, len(SECTIONS))
            odd = pe.value_load(odd_flag[0:1, 0:1])
            with pe.If(odd == 0):
                all_phases(exact=True)
            with pe.Else():
                pe.wait_ge(s_wlo, WCOLS // HID)
                all_phases(exact=False)


_OUT = ((P, NT, SUB, P), "float32")


def kernel(L0_attn_x, L0_attn_Wp, L0_attn_bp, L0_attn_Wo, L0_attn_bo, L0_attn_log_neg_lambdas, L0_attn_B_param,
           L0_attn_C_param, L0_attn_ln_gamma, L0_attn_ln_beta, L0_ffn_w1_w, L0_ffn_w1_s, L0_ffn_w2_w, L0_ffn_w2_s,
           L0_ffn_h1_w, L0_ffn_h1_s, L0_ffn_h2_w, L0_ffn_h2_s, L0_ffn_w3_w, L0_ffn_w3_s):
    import numpy as np
    import concourse.bacc as bacc
    from concourse.bass_utils import run_bass_kernel_spmd

    def blocks(w):
        w = np.asarray(w)
        o, i = w.shape
        return w.T.reshape(i // P, P, o).transpose(1, 0, 2).reshape(P, -1)

    def column(s):
        s = np.asarray(s).reshape(-1, P).T
        return np.concatenate([s, np.zeros((P, KB - s.shape[1]), s.dtype)], 1)

    arrays = {
        "x": np.asarray(L0_attn_x).reshape(NT, SUB, P, P).transpose(2, 0, 1, 3),
        "weights": np.concatenate([blocks(w) for w in (L0_ffn_w1_w, L0_ffn_w2_w, L0_ffn_h1_w, L0_ffn_h2_w,
                                                       L0_ffn_w3_w)], 1),
        "scales": np.stack([column(s) for s in (L0_ffn_w1_s, L0_ffn_w2_s, L0_ffn_h1_s, L0_ffn_h2_s,
                                                L0_ffn_w3_s)], 1),
        "rows": np.stack([np.asarray(v) for v in (L0_attn_bo, L0_attn_ln_gamma, L0_attn_ln_beta)]),
        "wp": np.asarray(L0_attn_Wp),
        "cmat": np.asarray(L0_attn_C_param),
        "wo": np.asarray(L0_attn_Wo),
        "chan": np.stack([np.asarray(v).reshape(-1) for v in (L0_attn_log_neg_lambdas, L0_attn_B_param,
                                                              L0_attn_bp)], 1),
    }
    nc = bacc.Bacc("TRN2", target_bir_lowering=False, num_devices=1)
    ins = {}
    aps = []
    for name, a in arrays.items():
        a = np.ascontiguousarray(a)
        ins[f"in_{name}"] = a
        aps.append(nc.dram_tensor(f"in_{name}", a.shape, mybir.dt.from_np(a.dtype), kind="ExternalInput").ap())
    out = nc.dram_tensor("out", _OUT[0], mybir.dt.from_np(np.dtype(_OUT[1])), kind="ExternalOutput").ap()
    macaron_kernel(nc, *aps, out)
    r = run_bass_kernel_spmd(nc, [ins], core_ids=[0])
    got = r.results[0]["out"]
    return got.transpose(1, 2, 0, 3).reshape(BATCH, SEQ, P)
```

```python
import concourse.bass as bass
from concourse import mybir
from contextlib import ExitStack

f32 = mybir.dt.float32
f32r = mybir.dt.float32r
u16 = mybir.dt.uint16
i32 = mybir.dt.int32
ALU = mybir.AluOpType
ACT = mybir.ActivationFunctionType
AX = mybir.AxisListType

P = 128
BATCH, SEQ = 16, 256
TOK = 512
NT = BATCH * SEQ // TOK
SUB = TOK // P
SB = TOK // SEQ
HID = 512
KB = HID // P
CH = 32
HEADS, DH = 2, 16
EPS = 1e-5
UNITS = 2 * NT

W1, W2 = 0, HID
H1, H2 = 2 * HID, 2 * HID + KB * HID
W3 = 2 * HID + 2 * KB * HID
WCOLS = W3 + KB * P
SECTIONS = [(W1, W2), (W2, H1), (H1, H2), (H2, W3), (W3, WCOLS)]

FIRST_CHECKS = 2
CHECKS = FIRST_CHECKS + 2 + KB + 1


def b_unit(t):
    if isinstance(t, int) and t >= NT - 2:
        return UNITS - NT + t
    return t * 2 + 3


HALVES = 2
HALF = TOK // HALVES
LAST = 2 * NT * 8 - 4

IDLE = 6
POOL_STEPS, DVE_STEPS = 14, 40


class Steps:

    def __init__(self, eng, sem):
        self.eng, self.sem, self.base, self.n = eng, sem, 0, 0

    def add(self, ins):
        self.n += 1
        ins.then_inc(self.sem, 1)
        return self.base + self.n

    def wait(self, value):
        self.eng.wait_ge(self.sem, value)

    def enter(self, i, first, per_turn):
        self.start, self.first, self.per_turn = self.base + self.n, first, per_turn
        self.base, self.n = (i - first) * per_turn + self.start, 0

    def leave(self, turns):
        assert self.n == self.per_turn, (self.n, self.per_turn)
        self.base, self.n = self.start + turns * self.per_turn, 0


class Phase:

    def __init__(self, n, finish=None, mix=None, prepare=None, norm=None, late=False, after=None,
                 stats=None):
        self.n, self.finish, self.mix, self.prepare = n, finish, mix, prepare
        self.norm, self.late = norm, late
        self.stats = stats
        self.after = after


HEAD_LATE = Phase(2, finish=("A", 1), mix=0, prepare=("B", 0), norm=0, late=True)
HEAD = [
    Phase(0, prepare=("A", 1), stats=2),
    Phase(1, finish=("A", 0), prepare=("A", 2)),
    HEAD_LATE,
    Phase(3, finish=("A", 2), mix=1, prepare=("A", 3), norm=1, after=HEAD_LATE, stats=3),
]
LOOP_FIRST, LOOP_END = 2, NT - 2


def loop_phases(i):
    return [
        Phase(i * 2, finish=("B", i - 2), mix=i, prepare=("B", i - 1), stats=i + 2),
        Phase(i * 2 + 1, finish=("A", i + 1), prepare=("A", i + 2), norm=i),
    ]


TAIL_LATE = Phase(2 * NT - 2, finish=("B", NT - 3), mix=NT - 1, prepare=("B", NT - 1), norm=NT - 1, late=True)
TAIL = [
    Phase(2 * NT - 4, finish=("B", NT - 4), mix=NT - 2, prepare=("B", NT - 3)),
    Phase(2 * NT - 3, finish=("A", NT - 1), prepare=("B", NT - 2), norm=NT - 2),
    TAIL_LATE,
    Phase(2 * NT - 1, finish=("B", NT - 2), after=TAIL_LATE),
]


def half_of(h):
    return slice(h * HALF, (h + 1) * HALF)


def tile_of(a, t):
    return a[:, t] if isinstance(t, int) else a[:, bass.ds(t, 1)].rearrange("p o s f -> p (o s) f")


def above(value, least):
    return not isinstance(value, int) or value >= least


def macaron_kernel(nc, x, weights, scales, rows, wp, cmat, wo, chan, out):
    ctx = ExitStack()
    with ctx:
        def sb(name, shape, dt=f32):
            return ctx.enter_context(nc.sbuf_tensor(name, shape, dt))

        def pb(name):
            return ctx.enter_context(nc.psum_tensor(name, [P, TOK], f32))

        def sem(name):
            return ctx.enter_context(nc.semaphore(name))

        w_raw = sb("w_raw", [P, WCOLS])
        w_hi = sb("w_hi", [P, WCOLS], f32r)
        w_lo = sb("w_lo", [P, WCOLS], f32r)
        low_half = sb("low_half", [P, 2 * HID], mybir.dt.bfloat16)
        odd_cols = sb("odd_cols", [P, CHECKS])
        odd_flag = sb("odd_flag", [1, 2], i32)
        ones_col = sb("ones_col", [P, 1])
        scale_in = sb("scale_in", [P, 5, KB])
        half_s1 = sb("half_s1", [P, KB])
        gate_s = sb("gate_s", [P, KB])
        half_s3 = sb("half_s3", [P, 1])
        row_in = sb("row_in", [P, 3, P])
        bo_bc, gamma_bc, beta_bc = (row_in[:, r, :] for r in range(3))
        bo4 = sb("bo4", [P, SUB, P])
        beta4 = sb("beta4", [P, SUB, P])
        ident = sb("ident", [P, P])
        wp_pad = sb("wp_pad", [P, SB, P])
        c_diag = sb("c_diag", [CH, SB, CH])
        wo_in = sb("wo_in", [CH, P])
        cwo = sb("cwo", [P, SB, P])
        chan_in = sb("chan_in", [SB * CH, 3])
        lam_t = sb("lam_t", [SB * CH, 1])
        lam = sb("lam", [SB * CH, SEQ])
        act_idle = sb("act_idle", [P, 1])
        pool_idle, dve_idle = sb("pool_idle", [P, IDLE]), sb("dve_idle", [P, IDLE])
        minus_half = sb("minus_half", [P, SUB])

        x_all = sb("x_all", [P, NT, SUB, P])
        x2_all = sb("x2_all", [P, NT, SUB, P])
        x1 = sb("x1", [P, SUB, P])
        x2 = sb("x2", [P, SUB, P])
        xn_a = sb("xn_a", [P, SUB, P])
        xn_b = sb("xn_b", [P, SUB, P])
        z = sb("z", [P, SUB, P])
        z_bo = sb("z_bo", [P, SUB, P])
        x1_beta = sb("x1_beta", [P, SUB, P])
        mixed = sb("mixed", [P, SUB, P])
        centred = sb("centred", [P, SUB, P])
        out_sb = sb("out_sb", [P, SUB, P])
        ln = {k: dict(stats=sb(f"stats_{k}", [P, SUB, 6]), mv=sb(f"mv_{k}", [P, SUB, 2]),
                      var=sb(f"var_{k}", [P, SUB]), neg=sb(f"neg_{k}", [P, SUB]), rstd=sb(f"rstd_{k}", [P, SUB])) for k in ("a", "z", "mix", "b")}
        xt_hi = sb("xt_hi", [P, TOK], f32r)
        xt_lo = sb("xt_lo", [P, TOK], f32r)
        z_t = sb("z_t", [P, TOK])
        tanh_g = sb("tanh_g", [P, 2, TOK])
        gate = sb("gate", [P, 2, TOK])
        h1f = sb("h1f", [P, 2, TOK])
        h1_hi = sb("h1_hi", [P, KB, TOK], f32r)
        h1_lo = sb("h1_lo", [P, KB, TOK], f32r)
        hf = sb("hf", [P, 2, TOK])
        h2_hi = sb("h2_hi", [P, KB, TOK], f32r)
        h2_lo = sb("h2_lo", [P, KB, TOK], f32r)
        h3_hi = sb("h3_hi", [P, KB, TOK], f32r)
        h3_lo = sb("h3_lo", [P, KB, TOK], f32r)
        y_t = sb("y_t", [P, TOK])
        u_in = sb("u_in", [SB * CH, SEQ])
        state = sb("state", [P, SEQ])

        ps_g = [pb(f"ps_g{j}") for j in range(2)]
        ps_u = [pb(f"ps_u{j}") for j in range(2)]
        ps_h = [pb(f"ps_h{j}") for j in range(2)]
        ps_y = pb("ps_y")
        ps_m = pb("ps_m")
        ps_last = [ps_g[0], ps_g[1], ps_h[0], ps_u[0], ps_u[1], ps_h[1], ps_g[0], ps_g[1]]
        ps_last_y = [ps_y, ps_m]

        s_x = [sem(f"x_loaded{t}") for t in range(2)]
        s_xrest = sem("x_rest_loaded")
        s_w = [sem(f"weights_loaded{j}") for j in range(len(SECTIONS))]
        s_scale = sem("scales_loaded")
        s_chan = sem("channels_loaded")
        s_par = sem("params_loaded")
        s_zero = sem("zeros_written")
        s_pad = sem("padded_loaded")
        s_ident = sem("ident_ready")
        s_const = sem("dve_consts_ready")
        s_whi = sem("w_hi_ready")
        s_check = sem("weights_checked")
        s_ones = sem("ones_ready")
        s_wlo = sem("w_lo_ready")
        s_wlo_first = sem("w_lo_of_layer1_ready")
        s_oddsum = sem("odd_sum_ready")
        s_flag = sem("flag_ready")
        s_half = sem("half_scales_ready")
        s_cwo_sb = sem("cwo_ready")
        s_cwo = sem("cwo_product_ready")
        s_lam = sem("lam_tanh_ready")
        s_xn_a = sem("xn_a_ready")
        s_xn_b = sem("xn_b_ready")
        s_xt = sem("xt_transposed")
        s_xt_hi = sem("xt_hi_ready")
        s_xt_lo = sem("xt_lo_ready")
        s_l1 = sem("l1_done")
        s_tanh = sem("tanh_ready")
        s_gate = sem("gate_ready")
        s_h1f = sem("h1f_ready")
        s_h1_hi = sem("h1_hi_ready")
        s_h1_lo = sem("h1_lo_ready")
        s_hid = sem("hidden_done")
        s_hid_hi = sem("hidden_hi_ready")
        s_hid_f = sem("hidden_full_ready")
        s_hid_lo = sem("hidden_lo_ready")
        s_y = sem("y_done")
        s_y_t = sem("y_scaled")
        s_yb = sem("y_transposed")
        s_fin = sem("y_added")
        s_z_st = sem("z_stats_ready")
        s_z = sem("z_ready")
        s_zbo = sem("z_bo_ready")
        s_x1b = sem("x1_beta_ready")
        s_zt = sem("z_transposed")
        s_zt_sb = sem("z_t_ready")
        s_xp = sem("xp_done")
        s_state = sem("state_ready")
        s_mix = sem("mix_product_done")
        s_mixed = sem("mixed_ready")
        s_mix_st = sem("mix_stats_ready")
        s_mix_r = sem("mix_rstd_ready")
        s_x2 = sem("x2_ready")
        s_b_st = sem("b_stats_ready")
        s_a_st = sem("a_stats_ready")
        s_a_r = sem("a_rstd_ready")
        s_stored = sem("out_stored")
        s_dve = sem("dve_steps")
        s_pool = sem("pool_steps")

        block = ctx.enter_context(nc.Block())

        @block.sync
        def _(sp):
            sp.dma_start(x_all[:, 0], x[:, 0]).then_inc(s_x[0], 16)
            for j, (a, b) in enumerate(SECTIONS):
                sp.dma_start(w_raw[:, a:b], weights[:, a:b]).then_inc(s_w[j], 16)
            sp.dma_start(x_all[:, 1], x[:, 1]).then_inc(s_x[1], 16)
            for r in range(3):
                sp.dma_start(row_in[:, r, :], rows[r:r + 1, :].to_broadcast([P, P])).then_inc(s_par, 16)
            sp.dma_start(wo_in[:], wo).then_inc(s_par, 16)
            sp.wait_ge(s_zero, 3)
            for b in range(SB):
                sp.dma_start(wp_pad[:, b, CH * b:CH * b + CH], wp).then_inc(s_pad, 16)
                for h in range(HEADS):
                    sp.dma_start(c_diag[DH * h:DH * h + DH, b, DH * h:DH * h + DH], cmat[h]).then_inc(s_pad, 16)
            sp.dma_start(x_all[:, 2:NT], x[:, 2:NT]).then_inc(s_xrest, 16)

            def store(t):
                sp.wait_ge(s_fin, b_unit(t) + 1)
                sp.dma_start(tile_of(out, t), out_sb[:]).then_inc(s_stored, 16)

            with sp.Fori(0, NT - 2) as t:
                store(t)
            store(NT - 2)
            for h in range(HALVES):
                sp.wait_ge(s_fin, UNITS + h)
                blocks = slice(h * SUB // HALVES, (h + 1) * SUB // HALVES)
                sp.dma_start(out[:, NT - 1, blocks], out_sb[:, blocks]).then_inc(s_stored, 16)
            sp.wait_ge(s_stored, 16 * (NT - 1 + HALVES))

        N_PAR = 16 * (3 + 1)
        N_PAD = 16 * SB * (1 + HEADS)

        @block.gpsimd
        def _(pool):
            st = Steps(pool, s_pool)
            nc.gpsimd.memset(minus_half[:], -0.5).then_inc(s_zero, 1)
            v = st.add(nc.gpsimd.memset(ident[:], 0.0))
            nc.gpsimd.memset(wp_pad[:], 0.0).then_inc(s_zero, 1)
            nc.gpsimd.memset(c_diag[:], 0.0).then_inc(s_zero, 1)
            st.wait(v)
            nc.gpsimd.affine_select(out=ident[:], in_=ident[:], compare_op=ALU.not_equal, fill=1.0, base=0,
                                    pattern=[[-1, P]], channel_multiplier=1).then_inc(s_ident, 1)


            idle = [0]

            def wait_alone(semaphore, value):
                pool.wait_ge(semaphore, value)
                if not isinstance(value, int):
                    idle[0] = (idle[0] + 1) % IDLE
                    nc.gpsimd.tensor_tensor(pool_idle[:, idle[0]:idle[0] + 1], minus_half[:, 0:1],
                                            minus_half[:, 1:2], ALU.add)


            def rstd(kind):
                c = ln[kind]
                v = st.add(nc.gpsimd.tensor_scalar(c["var"][:], c["mv"][:, :, 1], EPS, None, ALU.add))
                st.wait(v)
                return nc.gpsimd.tensor_tensor(c["rstd"][:], c["var"][:], minus_half[:], ALU.pow)

            def negate_mean(kind):
                c = ln[kind]
                return nc.gpsimd.tensor_scalar(c["neg"][:], c["mv"][:, :, 0], -1.0, None, ALU.mult)

            def normalise(kind, dst, src):
                c = ln[kind]
                for s in range(SUB):
                    last = nc.gpsimd.tensor_scalar(dst[:, s, :], src[:, s, :], c["neg"][:, s:s + 1],
                                                   c["rstd"][:, s:s + 1], ALU.add, ALU.mult)
                    if s < SUB - 1:
                        st.add(last)
                return last

            def rstd_a(count):
                wait_alone(s_a_st, count)
                rstd("a").then_inc(s_a_r, 1)

            def w_to_lo(sections, signal):
                for j in sections:
                    pool.wait_ge(s_whi, j + 1)
                    for c in range(*SECTIONS[j], HID):
                        nc.gpsimd.tensor_tensor(w_lo[:, c:c + HID], w_raw[:, c:c + HID],
                                                w_hi[:, c:c + HID].bitcast(f32), ALU.subtract).then_inc(signal, 1)

            def phase(ph):
                n = ph.n
                if ph.prepare and ph.prepare[0] == "A" and above(n, 1):
                    rstd_a(ph.prepare[1] + 1)
                if ph.mix is not None and ph.after:
                    add_bo(ph.mix)
                for k in range(KB):
                    pool.wait_ge(s_h1_hi, n * KB + k + 1)
                    if k == 0 and above(n, 1):
                        pool.wait_ge(s_hid, n * 8 - 4)
                    nc.gpsimd.tensor_tensor(h1_lo[:, k, :], h1f[:, k % 2, :], h1_hi[:, k, :].bitcast(f32),
                                            ALU.subtract).then_inc(s_h1_lo, 1)
                    if k == 1 and ph.mix is not None and not ph.after:
                        add_bo(ph.mix)
                if ph.mix is not None:
                    add_beta(ph.mix)
                if isinstance(n, int) and n == 0:
                    rstd_a(ph.prepare[1] + 1)
                if ph.norm is not None and ph.mix is None:
                    normalise_b(ph.norm)
                if isinstance(n, int) and n == 0:
                    pool.wait_ge(s_flag, 2)
                    odd = pool.value_load(odd_flag[0:1, 1:2])
                    with pool.If(odd != 0):
                        w_to_lo(range(len(SECTIONS)), s_wlo)
                if ph.mix is not None:
                    wait_alone(s_mix_st, ph.mix + 1)
                    rstd("mix").then_inc(s_mix_r, 1)
                    if ph.late:
                        normalise_b(ph.norm)
                if ph.finish and ph.finish[0] == "A":
                    t = ph.finish[1]
                    if above(t, 1):
                        pool.wait_ge(s_zt, t)
                    wait_alone(s_z_st, t + 1)
                    st.add(negate_mean("z"))
                    v = st.add(rstd("z"))
                    wait_alone(st.sem, v)
                    normalise("z", z, x1[:]).then_inc(s_z, 1)
                if ph.mix is not None and ph.norm is not None and not ph.late:
                    normalise_b(ph.norm)

            def normalise_b(t):
                if above(t, 1):
                    pool.wait_ge(s_xt, b_unit(t - 1) + 1)
                wait_alone(s_b_st, t + 1)
                st.add(negate_mean("b"))
                v = st.add(rstd("b"))
                wait_alone(st.sem, v)
                normalise("b", xn_b, x2).then_inc(s_xn_b, 1)

            def add_bo(t):
                pool.wait_ge(s_z, t + 1)
                if isinstance(t, int) and t == 0:
                    pool.wait_ge(s_const, 1)
                if above(t, 1):
                    pool.wait_ge(s_mixed, t)
                nc.gpsimd.tensor_tensor(z_bo[:], z[:], bo4[:], ALU.add).then_inc(s_zbo, 1)

            def add_beta(t):
                if above(t, 1):
                    pool.wait_ge(s_x2, t)
                nc.gpsimd.tensor_tensor(x1_beta[:], x1[:], beta4[:], ALU.add).then_inc(s_x1b, 1)

            rstd_a(1)
            pool.wait_ge(s_flag, 1)
            odd_first = pool.value_load(odd_flag[0:1, 0:1])
            with pool.If(odd_first != 0):
                w_to_lo(range(0, 2), s_wlo_first)

            for ph in HEAD:
                phase(ph)
            with pool.Fori(LOOP_FIRST, LOOP_END) as i:
                st.enter(i, LOOP_FIRST, POOL_STEPS)
                for ph in loop_phases(i):
                    phase(ph)
                st.leave(LOOP_END - LOOP_FIRST)
            for ph in TAIL:
                phase(ph)

        @block.scalar
        def _(act):
            act.dma_start(scale_in[:], scales).then_inc(s_scale, 16)
            for b in range(SB):
                act.dma_start(chan_in[CH * b:CH * b + CH, :], chan).then_inc(s_chan, 16)
            act.wait_ge(s_zero, 1)
            nc.scalar.activation(act_idle[:], minus_half[:, 0:1], ACT.Gelu).then_inc(s_lam, 1)

            def xt_to_hi(n):
                act.wait_ge(s_xt, n + 1)
                nc.scalar.activation(xt_hi[:], ps_m[:], ACT.Copy).then_inc(s_xt_hi, 1)

            def gelu_hi(q, k, scale, dst_hi):
                act.wait_ge(s_hid, q + 1)
                nc.scalar.activation(dst_hi, ps_h[k % 2][:], ACT.Gelu, scale=scale).then_inc(s_hid_hi, 1)

            def gelu_full(q, k, scale):
                if above(q, 2):
                    act.wait_ge(s_hid_lo, q - 1)
                nc.scalar.activation(hf[:, k % 2, :], ps_h[k % 2][:], ACT.Gelu, scale=scale).then_inc(s_hid_f, 1)

            def tanh(n, k):
                q = n * KB + k
                act.wait_ge(s_l1, q + 1)
                if above(q, 2):
                    act.wait_ge(s_gate, q - 1)
                nc.scalar.activation(tanh_g[:, k % 2, :], ps_g[k % 2][:], ACT.Tanh,
                                     scale=half_s1[:, k:k + 1]).then_inc(s_tanh, 1)

            def round_h1(n, k):
                act.wait_ge(s_h1f, n * KB + k + 1)
                nc.scalar.activation(h1_hi[:, k, :], h1f[:, k % 2, :], ACT.Copy).then_inc(s_h1_hi, 1)

            def gelu3_hi(n, k):
                gelu_hi(n * 8 - 4 + k, k, scale_in[:, 3, k:k + 1], h3_hi[:, k, :])

            def gelu3_full(n, k):
                gelu_full(n * 8 - 4 + k, k, scale_in[:, 3, k:k + 1])

            def gelu3(n, k):
                gelu3_hi(n, k)
                gelu3_full(n, k)

            def z_to_sbuf(t):
                act.wait_ge(s_zt, t + 1)
                nc.scalar.activation(z_t[:], ps_m[:], ACT.Copy).then_inc(s_zt_sb, 1)

            def phase(ph):
                n = ph.n
                if ph.after:
                    xt_to_hi(n)
                    gelu3(n, 0)
                    gelu3_hi(n, 1)
                    tanh(n, 0)
                    gelu3_full(n, 1)
                    tanh(n, 1)
                    round_h1(n, 0)
                    tanh(n, 2)
                    if ph.mix is not None:
                        z_to_sbuf(ph.mix)
                    round_h1(n, 1)
                    tanh(n, 3)
                    round_h1(n, 2)
                    gelu3(n, 2)
                    round_h1(n, 3)
                    gelu3(n, 3)
                elif ph.finish:
                    tanh(n, 0)
                    tanh(n, 1)
                    round_h1(n, 0)
                    gelu3(n, 0)
                    round_h1(n, 1)
                    tanh(n, 2)
                    if ph.mix is not None:
                        z_to_sbuf(ph.mix)
                    gelu3(n, 1)
                    tanh(n, 3)
                    round_h1(n, 2)
                    gelu3(n, 2)
                    round_h1(n, 3)
                    gelu3(n, 3)
                else:
                    tanh(n, 0)
                    check_weights(H2, H2 + HID, 3)
                    tanh(n, 1)
                    round_h1(n, 0)
                    tanh(n, 2)
                    check_weights(H2 + HID, H2 + 2 * HID, 3)
                    round_h1(n, 1)
                    tanh(n, 3)
                    check_weights(H2 + 2 * HID, H2 + 3 * HID, 3)
                    round_h1(n, 2)
                    check_weights(H2 + 3 * HID, W3, 3)
                    check_weights(W3, WCOLS, 4)
                    round_h1(n, 3)
                for k in range(KB):
                    gelu_hi(n * 8 + k, k, scale_in[:, 2, k:k + 1], h2_hi[:, k, :])
                    gelu_full(n * 8 + k, k, scale_in[:, 2, k:k + 1])
                    if k == 1 and ph.finish:
                        scale_y(n)
                    if k == 1 and ph.prepare and not ph.late:
                        xt_to_hi(n + 1)

            def last_phase():
                for h in range(HALVES):
                    for k in range(KB):
                        q, b = h * KB + k, half_of(h)
                        act.wait_ge(s_hid, LAST + q + 1)
                        nc.scalar.activation(h3_hi[:, k, b], ps_last[q][:, b], ACT.Gelu,
                                             scale=scale_in[:, 3, k:k + 1]).then_inc(s_hid_hi, 1)
                        act.wait_ge(s_hid_lo, LAST + q - 1)
                        nc.scalar.activation(hf[:, k % 2, b], ps_last[q][:, b], ACT.Gelu,
                                             scale=scale_in[:, 3, k:k + 1]).then_inc(s_hid_f, 1)
                for h in range(HALVES):
                    act.wait_ge(s_y, UNITS + h)
                    nc.scalar.activation(y_t[:, half_of(h)], ps_last_y[h][:, half_of(h)], ACT.Copy,
                                         scale=half_s3[:]).then_inc(s_y_t, 1)

            def scale_y(n):
                act.wait_ge(s_y, n)
                nc.scalar.activation(y_t[:], ps_y[:], ACT.Copy, scale=half_s3[:]).then_inc(s_y_t, 1)

            def check_weights(a, b, section):
                act.wait_ge(s_w[section], 16)
                low = w_raw[:, a:b].bitcast(u16).rearrange("p (n two) -> p n two", two=2)[:, :, 0]
                at = checks[0]
                checks[0] += 1
                nc.scalar.activation(low_half[:, 0:b - a], low, ACT.Copy,
                                     accum_out=odd_cols[:, at:at + 1]).then_inc(s_check, 1)
                act.wait_ge(s_check, at + 1)

            checks = [0]
            check_weights(W1, W2, 0)
            check_weights(W2, H1, 1)
            act.wait_ge(s_chan, 16 * SB)
            nc.scalar.activation(lam_t[:], chan_in[:, 0:1], ACT.Tanh, scale=0.5).then_inc(s_lam, 1)
            xt_to_hi(0)
            for c in range(H1, H2, 2 * HID):
                check_weights(c, c + 2 * HID, 2)
            act.wait_ge(s_half, 1)
            for ph in HEAD:
                phase(ph)
            with act.Fori(LOOP_FIRST, LOOP_END) as i:
                for ph in loop_phases(i):
                    phase(ph)
            for ph in TAIL:
                phase(ph)
            last_phase()

        @block.vector
        def _(dve):
            st = Steps(dve, s_dve)

            idle = [0]

            def wait_alone(semaphore, value):
                dve.wait_ge(semaphore, value)
                if not isinstance(value, int):
                    idle[0] = (idle[0] + 1) % IDLE
                    nc.vector.memset(dve_idle[:, idle[0]:idle[0] + 1], 0.0)


            def layer_stats(kind, src, first_wait=None):
                for s in range(SUB):
                    v = st.add(nc.vector.bn_stats(ln[kind]["stats"][:, s, :], src(s)))
                wait_alone(st.sem, v)
                for s in range(SUB):
                    last = nc.vector.bn_aggr(ln[kind]["mv"][:, s, :], ln[kind]["stats"][:, s, :])
                    if s < SUB - 1:
                        st.add(last)
                return last

            def stats_a(t):
                src = tile_of(x_all, t)
                layer_stats("a", lambda s: src[:, s, :]).then_inc(s_a_st, 1)

            def next_stats_a(t):
                dve.wait_ge(s_xrest, 16)
                stats_a(t)

            def normalise_a(t):
                dve.wait_ge(s_a_r, t + 1)
                dve.wait_ge(s_a_st, t + 1)
                src = tile_of(x_all, t)
                for s in range(SUB):
                    last = nc.vector.tensor_scalar(xn_a[:, s, :], src[:, s, :], ln["a"]["mv"][:, s, 0:1],
                                                   ln["a"]["rstd"][:, s:s + 1], ALU.subtract, ALU.mult)
                    if s < SUB - 1:
                        st.add(last)
                last.then_inc(s_xn_a, 1)

            def xt_to_lo(n):
                dve.wait_ge(s_xt_hi, n + 1)
                nc.vector.tensor_tensor(xt_lo[:], ps_m[:], xt_hi[:].bitcast(f32), ALU.subtract).then_inc(s_xt_lo, 1)

            def hidden_lo(q, k, hi, lo):
                dve.wait_ge(s_hid_f, q + 1)
                nc.vector.tensor_tensor(lo, hf[:, k % 2, :], hi.bitcast(f32), ALU.subtract).then_inc(s_hid_lo, 1)

            def recur(t):
                dve.wait_ge(s_xp, t + 1)
                v = st.add(nc.vector.tensor_scalar(u_in[:], ps_m[0:SB * CH, 0:SEQ], chan_in[:, 2:3], chan_in[:, 1:2],
                                                   ALU.add, ALU.mult))
                st.wait(v)
                nc.vector.tensor_tensor_scan(state[0:SB * CH, :], lam[:], u_in[:], 0.0, ALU.mult,
                                             ALU.add).then_inc(s_state, 1)

            def mixer_sum(t):
                dve.wait_ge(s_mix, t + 1)
                dve.wait_ge(s_zbo, t + 1)
                nc.vector.tensor_tensor(mixed[:], ps_m[:].rearrange("p (s f) -> p s f", s=SUB), z_bo[:],
                                        ALU.add).then_inc(s_mixed, 1)
                dve.wait_ge(s_mixed, t + 1)
                layer_stats("mix", lambda s: mixed[:, s, :]).then_inc(s_mix_st, 1)

            def mixer_norm(t):
                dve.wait_ge(s_mix_r, t + 1)
                dve.wait_ge(s_mix_st, t + 1)
                for s in range(SUB):
                    v = st.add(nc.vector.scalar_tensor_tensor(
                        out=centred[:, s, :], in0=mixed[:, s, :], scalar=ln["mix"]["mv"][:, s, 0:1], in1=gamma_bc,
                        op0=ALU.subtract, op1=ALU.mult))
                dve.wait_ge(s_x1b, t + 1)
                st.wait(v)
                if above(t, 1):
                    dve.wait_ge(s_xn_b, t)
                for s in range(SUB):
                    last = nc.vector.scalar_tensor_tensor(
                        out=x2[:, s, :], in0=centred[:, s, :], scalar=ln["mix"]["rstd"][:, s:s + 1],
                        in1=x1_beta[:, s, :], op0=ALU.mult, op1=ALU.add)
                    if s < SUB - 1:
                        st.add(last)
                last.then_inc(s_x2, 1)

            def b_stats(t):
                dve.wait_ge(s_x2, t + 1)
                layer_stats("b", lambda s: x2[:, s, :]).then_inc(s_b_st, 1)
                st.add(nc.vector.tensor_copy(tile_of(x2_all, t), x2[:]))

            def finish(kind, t, n):
                dve.wait_ge(s_yb, n)
                y = ps_y[:].rearrange("p (s f) -> p s f", s=SUB)
                if kind == "A":
                    if above(t, 1):
                        dve.wait_ge(s_x1b, t)
                    nc.vector.tensor_tensor(x1[:], y, tile_of(x_all, t), ALU.add).then_inc(s_fin, 1)
                else:
                    if above(t, 1):
                        dve.wait_ge(s_stored, t * 16)
                    nc.vector.tensor_tensor(out_sb[:], y, tile_of(x2_all, t), ALU.add).then_inc(s_fin, 1)

            def finish_stats(n):
                dve.wait_ge(s_fin, n)
                layer_stats("z", lambda s: x1[:, s, :]).then_inc(s_z_st, 1)

            def gated(n, k):
                q = n * KB + k
                dve.wait_ge(s_tanh, q + 1)
                nc.vector.scalar_tensor_tensor(
                    out=gate[:, k % 2, :], in0=tanh_g[:, k % 2, :], scalar=1.0, in1=ps_g[k % 2][:],
                    op0=ALU.add, op1=ALU.mult).then_inc(s_gate, 1)
                dve.wait_ge(s_gate, q + 1)
                if above(q, 2):
                    dve.wait_ge(s_h1_hi, q - 1)
                    dve.wait_ge(s_h1_lo, q - 1)
                nc.vector.scalar_tensor_tensor(
                    out=h1f[:, k % 2, :], in0=ps_u[k % 2][:], scalar=gate_s[:, k:k + 1], in1=gate[:, k % 2, :],
                    op0=ALU.mult, op1=ALU.mult).then_inc(s_h1f, 1)

            def lo3(n, k):
                hidden_lo(n * 8 - 4 + k, k, h3_hi[:, k, :], h3_lo[:, k, :])

            def lo2(n, k):
                hidden_lo(n * 8 + k, k, h2_hi[:, k, :], h2_lo[:, k, :])

            def round_weights(a, b, section):
                dve.wait_ge(s_w[section], 16)
                return nc.vector.tensor_copy(w_hi[:, a:b], w_raw[:, a:b])

            def make_flag(f, checks):
                dve.wait_ge(s_oddsum, f + 1)
                nc.vector.tensor_reduce(odd_flag[:, f:f + 1], ps_y[0:1, 0:checks], AX.X,
                                        ALU.max).then_inc(s_flag, 1)

            def phase(ph):
                n = ph.n
                prepare_a = ph.prepare[1] if ph.prepare and ph.prepare[0] == "A" else None

                if ph.finish:
                    if ph.after:
                        if ph.stats is not None:
                            next_stats_a(ph.stats)
                        xt_to_lo(n)
                        lo3(n, 0)
                    gated(n, 0)
                    gated(n, 1)
                    if ph.after:
                        lo3(n, 1)
                    else:
                        lo3(n, 0)
                    gated(n, 2)
                    gated(n, 3)
                    if ph.mix is not None:
                        recur(ph.mix)
                    if not ph.after:
                        lo3(n, 1)
                    if ph.mix is None and ph.norm is not None:
                        b_stats(ph.norm)
                    lo3(n, 2)
                    if ph.mix is not None:
                        mixer_sum(ph.mix)
                    lo3(n, 3)
                else:
                    st.add(round_weights(H2, H2 + 2 * HID, 3))
                    gated(n, 0)
                    gated(n, 1)
                    st.add(round_weights(H2 + 2 * HID, H2 + 3 * HID, 3))
                    gated(n, 2)
                    dve.wait_ge(s_cwo, 1)
                    for b in range(SB):
                        rows_b = slice(CH * b, CH * b + CH)
                        last = nc.vector.tensor_copy(cwo[rows_b, b, :], ps_y[rows_b, 0:P])
                        if b < SB - 1:
                            st.add(last)
                    last.then_inc(s_cwo_sb, 1)
                    gated(n, 3)
                    round_weights(H2 + 3 * HID, W3, 3).then_inc(s_whi, 1)
                    round_weights(W3, WCOLS, 4).then_inc(s_whi, 1)
                    make_flag(1, CHECKS)
                    dve.wait_ge(s_x[1], 16)
                    stats_a(1)
                    normalise_a(prepare_a)
                    dve.wait_ge(s_par, N_PAR)
                    st.add(nc.vector.tensor_copy(bo4[:], bo_bc.unsqueeze(1).broadcast_to([P, SUB, P])))
                    nc.vector.tensor_copy(beta4[:], beta_bc.unsqueeze(1).broadcast_to([P, SUB, P])).then_inc(s_const, 1)
                lo2(n, 0)
                if prepare_a is not None and ph.finish:
                    normalise_a(prepare_a)
                if ph.mix is not None:
                    mixer_norm(ph.mix)
                    if ph.late:
                        b_stats(ph.norm)
                lo2(n, 1)
                if ph.prepare and not ph.late:
                    xt_to_lo(n + 1)
                if ph.stats is not None and not ph.after:
                    next_stats_a(ph.stats)
                if ph.finish and ph.finish[0] == "A" and not ph.late:
                    finish(*ph.finish, n)
                    finish_stats(n)
                    lo2(n, 2)
                else:
                    lo2(n, 2)
                    if ph.finish:
                        finish(*ph.finish, n)
                if ph.mix is not None and ph.norm is not None and not ph.late:
                    b_stats(ph.norm)
                lo2(n, 3)
                if ph.finish and ph.finish[0] == "A" and ph.late:
                    finish_stats(n)

            def last_phase():
                for h in range(HALVES):
                    for k in range(KB):
                        b = half_of(h)
                        dve.wait_ge(s_hid_f, LAST + h * KB + k + 1)
                        nc.vector.tensor_tensor(h3_lo[:, k, b], hf[:, k % 2, b], h3_hi[:, k, b].bitcast(f32),
                                                ALU.subtract).then_inc(s_hid_lo, 1)
                dve.wait_ge(s_stored, (NT - 1) * 16)
                for h in range(HALVES):
                    blocks = slice(h * SUB // HALVES, (h + 1) * SUB // HALVES)
                    dve.wait_ge(s_yb, UNITS + h)
                    nc.vector.tensor_tensor(out_sb[:, blocks], ps_last_y[h][:, half_of(h)].rearrange("p (s f) -> p s f", f=P),
                                            x2_all[:, NT - 1, blocks], ALU.add).then_inc(s_fin, 1)

            st.add(nc.vector.memset(ones_col[:], 1.0))
            st.add(nc.vector.memset(state[:], 0.0))
            st.add(nc.vector.memset(cwo[:], 0.0))
            nc.vector.memset(lam[:], 1.0).then_inc(s_ones, 1)
            dve.wait_ge(s_scale, 16)
            v = st.add(nc.vector.tensor_scalar(half_s1[:], scale_in[:, 0, :], 0.5, None, ALU.mult))
            nc.vector.tensor_scalar(half_s3[:], scale_in[:, 4, 0:1], 0.5, None, ALU.mult).then_inc(s_half, 1)
            st.wait(v)
            st.add(nc.vector.tensor_tensor(gate_s[:], half_s1[:], scale_in[:, 1, :], ALU.mult))
            dve.wait_ge(s_x[0], 16)
            stats_a(0)
            round_weights(W1, W2, 0).then_inc(s_whi, 1)
            round_weights(W2, H1, 1).then_inc(s_whi, 1)
            make_flag(0, FIRST_CHECKS)
            normalise_a(0)
            xt_to_lo(0)
            round_weights(H1, H2, 2).then_inc(s_whi, 1)
            dve.wait_ge(s_lam, 2)
            v = st.add(nc.vector.tensor_scalar(lam_t[:], lam_t[:], 0.5, 0.5, ALU.mult, ALU.add))
            st.wait(v)
            st.add(nc.vector.tensor_scalar(lam[:], lam[:], lam_t[:], None, ALU.mult))

            for ph in HEAD:
                phase(ph)
            with dve.Fori(LOOP_FIRST, LOOP_END) as i:
                st.enter(i, LOOP_FIRST, DVE_STEPS)
                for ph in loop_phases(i):
                    phase(ph)
                st.leave(LOOP_END - LOOP_FIRST)
            for ph in TAIL:
                phase(ph)
            last_phase()

        @block.tensor
        def _(pe):
            def transpose4(dst, src):
                for s in range(SUB):
                    last = nc.tensor.transpose(dst[:, s * P:(s + 1) * P], src(s), ident[:])
                return last

            def product(dst, wcol, hi, lo, first, final, exact, lo_wait=None):
                w = w_hi[:, wcol:wcol + P]
                nc.tensor.matmul(dst, w, hi, start=first, stop=False)
                if not exact:
                    nc.tensor.matmul(dst, w_lo[:, wcol:wcol + P], hi, start=False, stop=False)
                if lo_wait:
                    pe.wait_ge(*lo_wait)
                last = nc.tensor.matmul(dst, w, lo, start=False, stop=final and exact)
                if not exact:
                    last = nc.tensor.matmul(dst, w_lo[:, wcol:wcol + P], lo, start=False, stop=final)
                return last

            def transpose_input(n, src, ready, count):
                pe.wait_ge(ready, count)
                transpose4(ps_m, lambda s: src[:, s, :]).then_inc(s_xt, 1)

            def layer1(n, k, exact):
                q = n * KB + k
                if k == 0:
                    pe.wait_ge(s_xt_hi, n + 1)
                if above(q, 2):
                    pe.wait_ge(s_gate, q - 1)
                product(ps_g[k % 2][:], W1 + k * P, xt_hi[:], xt_lo[:], True, True, exact,
                        (s_xt_lo, n + 1) if k == 0 else None)
                if above(q, 2):
                    pe.wait_ge(s_h1f, q - 1)
                product(ps_u[k % 2][:], W2 + k * P, xt_hi[:], xt_lo[:], True, True, exact).then_inc(s_l1, 1)

            def hidden(q, k, w0, hi, lo, hi_at, lo_at, exact):
                if above(q, 2):
                    pe.wait_ge(s_hid_f, q - 1)
                for j in range(KB):
                    if k == 0:
                        pe.wait_ge(hi_at[0], hi_at[1] + j + 1)
                    last = product(ps_h[k % 2][:], w0 + j * HID + k * P, hi[:, j, :], lo[:, j, :],
                                   j == 0, j == KB - 1, exact,
                                   (lo_at[0], lo_at[1] + j + 1) if k == 0 else None)
                last.then_inc(s_hid, 1)

            def last_layer(n, exact):
                if above(n, 2):
                    pe.wait_ge(s_fin, n - 1)
                for j in range(KB):
                    pe.wait_ge(s_hid_hi, n * 8 - 3 + j)
                    last = product(ps_y[:], W3 + j * P, h3_hi[:, j, :], h3_lo[:, j, :], j == 0, j == KB - 1, exact,
                                   (s_hid_lo, n * 8 - 3 + j))
                last.then_inc(s_y, 1)

            def transpose_y(n):
                pe.wait_ge(s_y_t, n)
                transpose4(ps_y, lambda s: y_t[:, s * P:(s + 1) * P]).then_inc(s_yb, 1)

            def z_transpose(t):
                pe.wait_ge(s_z, t + 1)
                transpose4(ps_m, lambda s: z[:, s, :]).then_inc(s_zt, 1)

            def project(t):
                pe.wait_ge(s_zt_sb, t + 1)
                for b in range(SB):
                    last = nc.tensor.matmul(ps_m[:, 0:SEQ], wp_pad[:, b, :], z_t[:, b * SEQ:(b + 1) * SEQ],
                                            start=b == 0, stop=b == SB - 1)
                last.then_inc(s_xp, 1)

            def mix_out(t):
                pe.wait_ge(s_state, t + 1)
                dst = ps_m[:].rearrange("p (b h f) -> p b h f", b=SB, h=SUB // SB)
                for h in range(SUB // SB):
                    last = nc.tensor.matmul(dst[:, :, h, :], state[:, h * P:(h + 1) * P], cwo[:],
                                            start=h == 0, stop=h == SUB // SB - 1, skip_group_check=True)
                last.then_inc(s_mix, 1)

            def prepare(ph):
                kind, t = ph.prepare
                if ph.mix is not None:
                    pe.wait_ge(s_mixed, ph.mix + 1)
                if kind == "A":
                    transpose_input(ph.n + 1, xn_a, s_xn_a, t + 1)
                else:
                    transpose_input(ph.n + 1, xn_b, s_xn_b, t + 1)

            def layer3(n, k, exact):
                hidden(n * 8 - 4 + k, k, H2, h2_hi, h2_lo, (s_hid_hi, n * 8 - 8), (s_hid_lo, n * 8 - 8), exact)

            def first_half(ph, exact):
                n = ph.n
                if ph.after:
                    layer3(n, 0, exact)
                    prepare(ph.after)
                    layer3(n, 1, exact)
                    layer1(n, 0, exact)
                    layer1(n, 1, exact)
                    if ph.mix is not None:
                        z_transpose(ph.mix)
                    layer1(n, 2, exact)
                    layer1(n, 3, exact)
                    layer3(n, 2, exact)
                    if ph.mix is not None:
                        project(ph.mix)
                    layer3(n, 3, exact)
                    if ph.mix is not None:
                        mix_out(ph.mix)
                elif ph.finish:
                    layer1(n, 0, exact)
                    layer1(n, 1, exact)
                    layer3(n, 0, exact)
                    layer1(n, 2, exact)
                    if ph.mix is not None:
                        z_transpose(ph.mix)
                    layer3(n, 1, exact)
                    layer1(n, 3, exact)
                    layer3(n, 2, exact)
                    if ph.mix is not None:
                        project(ph.mix)
                    layer3(n, 3, exact)
                    if ph.mix is not None:
                        mix_out(ph.mix)
                else:
                    for k in range(KB):
                        layer1(n, k, exact)

            def second_half(ph, exact):
                n = ph.n
                for k in range(KB):
                    hidden(n * 8 + k, k, H1, h1_hi, h1_lo, (s_h1_hi, n * KB), (s_h1_lo, n * KB), exact)
                    if k == 1 and ph.finish:
                        last_layer(n, exact)
                    if ph.prepare and k == 1 and not ph.late:
                        prepare(ph)
                    if k == 2 and ph.finish:
                        transpose_y(n)

            def phase(ph, exact):
                first_half(ph, exact)
                second_half(ph, exact)

            def last_phase(exact):
                bank_read = [(s_h1f, UNITS * KB), (s_h1f, UNITS * KB), (s_hid_f, LAST - 1), (s_h1f, UNITS * KB),
                             (s_h1f, UNITS * KB), (s_hid_f, LAST), (s_hid_f, LAST + 1), (s_hid_f, LAST + 2)]
                for h in range(HALVES):
                    b = half_of(h)
                    for js in ((range(KB - 1), range(KB - 1, KB)) if h == 0 else (range(KB),)):
                        for k in range(KB):
                            q = h * KB + k
                            if js[0] == 0:
                                pe.wait_ge(*bank_read[q])
                            for j in js:
                                pe.wait_ge(s_hid_hi, LAST - KB + j + 1)
                                last = product(ps_last[q][:, b], H2 + j * HID + k * P, h2_hi[:, j, b], h2_lo[:, j, b],
                                               j == 0, j == KB - 1, exact,
                                               (s_hid_lo, LAST - KB + j + 1))
                            if js[-1] == KB - 1:
                                last.then_inc(s_hid, 1)
                pe.wait_ge(s_fin, UNITS - 1)
                for h in range(HALVES):
                    b = half_of(h)
                    for j in range(KB):
                        pe.wait_ge(s_hid_hi, LAST + h * KB + j + 1)
                        last = product(ps_last_y[h][:, b], W3 + j * P, h3_hi[:, j, b], h3_lo[:, j, b], j == 0, j == KB - 1,
                                       exact, (s_hid_lo, LAST + h * KB + j + 1))
                    last.then_inc(s_y, 1)
                for h in range(HALVES):
                    pe.wait_ge(s_y_t, UNITS + h)
                    for c in range(h * HALF, (h + 1) * HALF, P):
                        last = nc.tensor.transpose(ps_last_y[h][:, c:c + P], y_t[:, c:c + P], ident[:])
                    last.then_inc(s_yb, 1)

            def all_phases(exact):
                second_half(HEAD[0], exact)
                for ph in HEAD[1:]:
                    phase(ph, exact)
                with pe.Fori(LOOP_FIRST, LOOP_END) as i:
                    for ph in loop_phases(i):
                        phase(ph, exact)
                for ph in TAIL:
                    phase(ph, exact)
                last_phase(exact)

            def sum_checks(checks):
                pe.wait_ge(s_check, checks)
                nc.tensor.matmul(ps_y[0:1, 0:checks], ones_col[:], odd_cols[:, 0:checks], start=True,
                                 stop=True).then_inc(s_oddsum, 1)

            pe.wait_ge(s_ones, 1)
            sum_checks(FIRST_CHECKS)
            pe.wait_ge(s_ident, 1)
            transpose_input(0, xn_a, s_xn_a, 1)
            pe.wait_ge(s_whi, 2)
            pe.wait_ge(s_flag, 1)
            odd_first = pe.value_load(odd_flag[0:1, 0:1])
            with pe.If(odd_first == 0):
                first_half(HEAD[0], exact=True)
            with pe.Else():
                pe.wait_ge(s_wlo_first, 2)
                first_half(HEAD[0], exact=False)
            pe.wait_ge(s_pad, N_PAD)
            pe.wait_ge(s_par, N_PAR)
            nc.tensor.matmul(ps_y[0:SB * CH, 0:P], c_diag[:].rearrange("k b d -> k (b d)"), wo_in[:], start=True,
                             stop=True).then_inc(s_cwo, 1)
            pe.wait_ge(s_cwo_sb, 1)
            sum_checks(CHECKS)
            pe.wait_ge(s_flag, 2)
            pe.wait_ge(s_whi, len(SECTIONS))
            odd = pe.value_load(odd_flag[0:1, 1:2])
            with pe.If(odd == 0):
                all_phases(exact=True)
            with pe.Else():
                pe.wait_ge(s_wlo, WCOLS // HID)
                all_phases(exact=False)


_OUT = ((P, NT, SUB, P), "float32")


def kernel(L0_attn_x, L0_attn_Wp, L0_attn_bp, L0_attn_Wo, L0_attn_bo, L0_attn_log_neg_lambdas, L0_attn_B_param,
           L0_attn_C_param, L0_attn_ln_gamma, L0_attn_ln_beta, L0_ffn_w1_w, L0_ffn_w1_s, L0_ffn_w2_w, L0_ffn_w2_s,
           L0_ffn_h1_w, L0_ffn_h1_s, L0_ffn_h2_w, L0_ffn_h2_s, L0_ffn_w3_w, L0_ffn_w3_s):
    import numpy as np
    import concourse.bacc as bacc
    from concourse.bass_utils import run_bass_kernel_spmd

    def blocks(w):
        w = np.asarray(w)
        o, i = w.shape
        return w.T.reshape(i // P, P, o).transpose(1, 0, 2).reshape(P, -1)

    def column(s):
        s = np.asarray(s).reshape(-1, P).T
        return np.concatenate([s, np.zeros((P, KB - s.shape[1]), s.dtype)], 1)

    arrays = {
        "x": np.asarray(L0_attn_x).reshape(NT, SUB, P, P).transpose(2, 0, 1, 3),
        "weights": np.concatenate([blocks(w) for w in (L0_ffn_w1_w, L0_ffn_w2_w, L0_ffn_h1_w, L0_ffn_h2_w,
                                                       L0_ffn_w3_w)], 1),
        "scales": np.stack([column(s) for s in (L0_ffn_w1_s, L0_ffn_w2_s, L0_ffn_h1_s, L0_ffn_h2_s,
                                                L0_ffn_w3_s)], 1),
        "rows": np.stack([np.asarray(v) for v in (L0_attn_bo, L0_attn_ln_gamma, L0_attn_ln_beta)]),
        "wp": np.asarray(L0_attn_Wp),
        "cmat": np.asarray(L0_attn_C_param),
        "wo": np.asarray(L0_attn_Wo),
        "chan": np.stack([np.asarray(v).reshape(-1) for v in (L0_attn_log_neg_lambdas, L0_attn_B_param,
                                                              L0_attn_bp)], 1),
    }
    nc = bacc.Bacc("TRN2", target_bir_lowering=False, num_devices=1)
    ins = {}
    aps = []
    for name, a in arrays.items():
        a = np.ascontiguousarray(a)
        ins[f"in_{name}"] = a
        aps.append(nc.dram_tensor(f"in_{name}", a.shape, mybir.dt.from_np(a.dtype), kind="ExternalInput").ap())
    out = nc.dram_tensor("out", _OUT[0], mybir.dt.from_np(np.dtype(_OUT[1])), kind="ExternalOutput").ap()
    macaron_kernel(nc, *aps, out)
    r = run_bass_kernel_spmd(nc, [ins], core_ids=[0])
    got = r.results[0]["out"]
    return got.transpose(1, 2, 0, 3).reshape(BATCH, SEQ, P)
```
